# Optimizing a Trainium2 kernel written in Bass

```python
import numpy as np
import jax
import jax.numpy as jnp

def _softmax(x, axis=-1):
    return jax.nn.softmax(x, axis=axis)

def _gelu(x):
    return jax.nn.gelu(x, approximate=True)

def _silu(x):
    return jax.nn.silu(x)

def _sigmoid(x):
    return jax.nn.sigmoid(x)

def _layernorm(x, axis=-1, eps=1e-05):
    m = jnp.mean(x, axis=axis, keepdims=True)
    v = jnp.var(x, axis=axis, keepdims=True)
    return (x - m) / jnp.sqrt(v + eps)

def _scatter_add(tgt, idx, src, axis=0):
    return tgt.at[idx].add(src)

def _segment_sum(src, seg, n):
    return jax.ops.segment_sum(src, seg, n)
kernel_name = 'mk_dlrm_tower_d1_rec_r8_01dc1e'

def setup_inputs(seed: int=0):
    np.random.seed(seed)
    _w = jnp.asarray

    def _rec_inputs():
        import jax
        import jax.numpy as jnp
        _tk = jax.random.key(seed)
        dense_ctx = jax.random.normal(jax.random.fold_in(_tk, 190), (1024, 16), jnp.float32)
        ids = jnp.stack([jax.random.randint(jax.random.fold_in(_tk, 200 + f), (1024,), 0, v, jnp.int32) for f, v in enumerate([125000, 1250, 1000, 125000, 125000, 1250, 12500, 1250, 1000, 1000, 1250, 125000, 1250, 12500, 1250, 1250, 1000, 1000, 12500, 125000, 125000, 1250, 125000, 125000, 12500, 125000, 125000, 125000, 12500, 125000, 12500, 1000])], axis=1)
        tbl_0 = 0.05 * jax.random.normal(jax.random.fold_in(_tk, 500 + 0), (125000, 16), jnp.float32)
        tbl_1 = 0.05 * jax.random.normal(jax.random.fold_in(_tk, 500 + 1), (1250, 16), jnp.float32)
        tbl_2 = 0.05 * jax.random.normal(jax.random.fold_in(_tk, 500 + 2), (1000, 16), jnp.float32)
        tbl_3 = 0.05 * jax.random.normal(jax.random.fold_in(_tk, 500 + 3), (125000, 16), jnp.float32)
        tbl_4 = 0.05 * jax.random.normal(jax.random.fold_in(_tk, 500 + 4), (125000, 16), jnp.float32)
        tbl_5 = 0.05 * jax.random.normal(jax.random.fold_in(_tk, 500 + 5), (1250, 16), jnp.float32)
        tbl_6 = 0.05 * jax.random.normal(jax.random.fold_in(_tk, 500 + 6), (12500, 16), jnp.float32)
        tbl_7 = 0.05 * jax.random.normal(jax.random.fold_in(_tk, 500 + 7), (1250, 16), jnp.float32)
        tbl_8 = 0.05 * jax.random.normal(jax.random.fold_in(_tk, 500 + 8), (1000, 16), jnp.float32)
        tbl_9 = 0.05 * jax.random.normal(jax.random.fold_in(_tk, 500 + 9), (1000, 16), jnp.float32)
        tbl_10 = 0.05 * jax.random.normal(jax.random.fold_in(_tk, 500 + 10), (1250, 16), jnp.float32)
        tbl_11 = 0.05 * jax.random.normal(jax.random.fold_in(_tk, 500 + 11), (125000, 16), jnp.float32)
        tbl_12 = 0.05 * jax.random.normal(jax.random.fold_in(_tk, 500 + 12), (1250, 16), jnp.float32)
        tbl_13 = 0.05 * jax.random.normal(jax.random.fold_in(_tk, 500 + 13), (12500, 16), jnp.float32)
        tbl_14 = 0.05 * jax.random.normal(jax.random.fold_in(_tk, 500 + 14), (1250, 16), jnp.float32)
        tbl_15 = 0.05 * jax.random.normal(jax.random.fold_in(_tk, 500 + 15), (1250, 16), jnp.float32)
        tbl_16 = 0.05 * jax.random.normal(jax.random.fold_in(_tk, 500 + 16), (1000, 16), jnp.float32)
        tbl_17 = 0.05 * jax.random.normal(jax.random.fold_in(_tk, 500 + 17), (1000, 16), jnp.float32)
        tbl_18 = 0.05 * jax.random.normal(jax.random.fold_in(_tk, 500 + 18), (12500, 16), jnp.float32)
        tbl_19 = 0.05 * jax.random.normal(jax.random.fold_in(_tk, 500 + 19), (125000, 16), jnp.float32)
        tbl_20 = 0.05 * jax.random.normal(jax.random.fold_in(_tk, 500 + 20), (125000, 16), jnp.float32)
        tbl_21 = 0.05 * jax.random.normal(jax.random.fold_in(_tk, 500 + 21), (1250, 16), jnp.float32)
        tbl_22 = 0.05 * jax.random.normal(jax.random.fold_in(_tk, 500 + 22), (125000, 16), jnp.float32)
        tbl_23 = 0.05 * jax.random.normal(jax.random.fold_in(_tk, 500 + 23), (125000, 16), jnp.float32)
        tbl_24 = 0.05 * jax.random.normal(jax.random.fold_in(_tk, 500 + 24), (12500, 16), jnp.float32)
        tbl_25 = 0.05 * jax.random.normal(jax.random.fold_in(_tk, 500 + 25), (125000, 16), jnp.float32)
        tbl_26 = 0.05 * jax.random.normal(jax.random.fold_in(_tk, 500 + 26), (125000, 16), jnp.float32)
        tbl_27 = 0.05 * jax.random.normal(jax.random.fold_in(_tk, 500 + 27), (125000, 16), jnp.float32)
        tbl_28 = 0.05 * jax.random.normal(jax.random.fold_in(_tk, 500 + 28), (12500, 16), jnp.float32)
        tbl_29 = 0.05 * jax.random.normal(jax.random.fold_in(_tk, 500 + 29), (125000, 16), jnp.float32)
        tbl_30 = 0.05 * jax.random.normal(jax.random.fold_in(_tk, 500 + 30), (12500, 16), jnp.float32)
        tbl_31 = 0.05 * jax.random.normal(jax.random.fold_in(_tk, 500 + 31), (1000, 16), jnp.float32)
        _rk = jax.random.fold_in(_tk, 7)
        W_top1 = 0.0606339 * jax.random.normal(jax.random.fold_in(_tk, 801), (272, 512), jnp.float32)
        W_top2 = 0.0441942 * jax.random.normal(jax.random.fold_in(_tk, 802), (512, 256), jnp.float32)
        W_top3 = 0.0625 * jax.random.normal(jax.random.fold_in(_tk, 803), (256, 1), jnp.float32)
        b_top1 = jnp.zeros((512,), jnp.float32)
        b_top2 = jnp.zeros((256,), jnp.float32)
        return (dense_ctx, ids, tbl_0, tbl_1, tbl_2, tbl_3, tbl_4, tbl_5, tbl_6, tbl_7, tbl_8, tbl_9, tbl_10, tbl_11, tbl_12, tbl_13, tbl_14, tbl_15, tbl_16, tbl_17, tbl_18, tbl_19, tbl_20, tbl_21, tbl_22, tbl_23, tbl_24, tbl_25, tbl_26, tbl_27, tbl_28, tbl_29, tbl_30, tbl_31, W_top1, b_top1, W_top2, b_top2, W_top3)
    dense_ctx, ids, tbl_0, tbl_1, tbl_2, tbl_3, tbl_4, tbl_5, tbl_6, tbl_7, tbl_8, tbl_9, tbl_10, tbl_11, tbl_12, tbl_13, tbl_14, tbl_15, tbl_16, tbl_17, tbl_18, tbl_19, tbl_20, tbl_21, tbl_22, tbl_23, tbl_24, tbl_25, tbl_26, tbl_27, tbl_28, tbl_29, tbl_30, tbl_31, W_top1, b_top1, W_top2, b_top2, W_top3 = _rec_inputs()

    def _L0_rec_setup():
        import jax, jax.numpy as jnp
        import numpy as np
        NUM_FIELDS = 32
        EMBED_DIM = 16
        BATCH = 512
        CROSS_SIZES = [128, 128, 128]

        def _cin_forward(x, Ws, bs):
            x0 = x
            h = x
            xs = []
            n_layers = len(Ws)
            for i in range(n_layers):
                B, F, E = x0.shape
                G = h.shape[1]
                z = (x0[:, :, None, :] * h[:, None, :, :]).reshape(B, F * G, E)
                y = jax.nn.relu(jnp.einsum('oc,bce->boe', Ws[i], z) + bs[i][None, :, None])
                if i != n_layers - 1:
                    half = y.shape[1] // 2
                    x_keep, h = (y[:, :half, :], y[:, half:, :])
                else:
                    x_keep, h = (y, y)
                xs.append(x_keep)
            return jnp.sum(jnp.concatenate(xs, axis=1), axis=2)
        key = jax.random.key(seed)
        ks = jax.random.split(key, 8)
        x = jax.random.normal(ks[0], (BATCH, NUM_FIELDS, EMBED_DIM), dtype=jnp.float32)
        prev = NUM_FIELDS
        inp = {'x': x}
        for i, cs in enumerate(CROSS_SIZES):
            in_ch = NUM_FIELDS * prev
            scale = 1.0 / np.sqrt(in_ch)
            inp[f'W{i}'] = jax.random.uniform(ks[1 + 2 * i], (cs, in_ch), dtype=jnp.float32, minval=-scale, maxval=scale)
            inp[f'b{i}'] = jax.random.uniform(ks[2 + 2 * i], (cs,), dtype=jnp.float32, minval=-scale, maxval=scale)
            prev = cs // 2
        return inp
    _L0_rec_all = _L0_rec_setup()
    _L0_rec_in = {k: v for k, v in _L0_rec_all.items() if k in ('W0', 'b0', 'W1', 'b1', 'W2', 'b2')}
    del _L0_rec_all
    return {'dense_ctx': dense_ctx, 'ids': ids, 'tbl_0': tbl_0, 'tbl_1': tbl_1, 'tbl_2': tbl_2, 'tbl_3': tbl_3, 'tbl_4': tbl_4, 'tbl_5': tbl_5, 'tbl_6': tbl_6, 'tbl_7': tbl_7, 'tbl_8': tbl_8, 'tbl_9': tbl_9, 'tbl_10': tbl_10, 'tbl_11': tbl_11, 'tbl_12': tbl_12, 'tbl_13': tbl_13, 'tbl_14': tbl_14, 'tbl_15': tbl_15, 'tbl_16': tbl_16, 'tbl_17': tbl_17, 'tbl_18': tbl_18, 'tbl_19': tbl_19, 'tbl_20': tbl_20, 'tbl_21': tbl_21, 'tbl_22': tbl_22, 'tbl_23': tbl_23, 'tbl_24': tbl_24, 'tbl_25': tbl_25, 'tbl_26': tbl_26, 'tbl_27': tbl_27, 'tbl_28': tbl_28, 'tbl_29': tbl_29, 'tbl_30': tbl_30, 'tbl_31': tbl_31, 'W_top1': W_top1, 'b_top1': b_top1, 'W_top2': W_top2, 'b_top2': b_top2, 'W_top3': W_top3, 'L0_rec_W0': _L0_rec_in['W0'], 'L0_rec_b0': _L0_rec_in['b0'], 'L0_rec_W1': _L0_rec_in['W1'], 'L0_rec_b1': _L0_rec_in['b1'], 'L0_rec_W2': _L0_rec_in['W2'], 'L0_rec_b2': _L0_rec_in['b2']}

def reference(dense_ctx, ids, tbl_0, tbl_1, tbl_2, tbl_3, tbl_4, tbl_5, tbl_6, tbl_7, tbl_8, tbl_9, tbl_10, tbl_11, tbl_12, tbl_13, tbl_14, tbl_15, tbl_16, tbl_17, tbl_18, tbl_19, tbl_20, tbl_21, tbl_22, tbl_23, tbl_24, tbl_25, tbl_26, tbl_27, tbl_28, tbl_29, tbl_30, tbl_31, W_top1, b_top1, W_top2, b_top2, W_top3, L0_rec_W0, L0_rec_b0, L0_rec_W1, L0_rec_b1, L0_rec_W2, L0_rec_b2):
    import jax
    import jax.numpy as jnp

    def _L0_rec_ref(x, W0, b0, W1, b1, W2, b2):
        import jax, jax.numpy as jnp
        import numpy as np
        NUM_FIELDS = 32
        EMBED_DIM = 16
        BATCH = 512
        CROSS_SIZES = [128, 128, 128]

        def _cin_forward(x, Ws, bs):
            x0 = x
            h = x
            xs = []
            n_layers = len(Ws)
            for i in range(n_layers):
                B, F, E = x0.shape
                G = h.shape[1]
                z = (x0[:, :, None, :] * h[:, None, :, :]).reshape(B, F * G, E)
                y = jax.nn.relu(jnp.einsum('oc,bce->boe', Ws[i], z) + bs[i][None, :, None])
                if i != n_layers - 1:
                    half = y.shape[1] // 2
                    x_keep, h = (y[:, :half, :], y[:, half:, :])
                else:
                    x_keep, h = (y, y)
                xs.append(x_keep)
            return jnp.sum(jnp.concatenate(xs, axis=1), axis=2)
        return _cin_forward(x, [W0, W1, W2], [b0, b1, b2])
    e = jnp.stack([tbl_0[ids[:, 0]], tbl_1[ids[:, 1]], tbl_2[ids[:, 2]], tbl_3[ids[:, 3]], tbl_4[ids[:, 4]], tbl_5[ids[:, 5]], tbl_6[ids[:, 6]], tbl_7[ids[:, 7]], tbl_8[ids[:, 8]], tbl_9[ids[:, 9]], tbl_10[ids[:, 10]], tbl_11[ids[:, 11]], tbl_12[ids[:, 12]], tbl_13[ids[:, 13]], tbl_14[ids[:, 14]], tbl_15[ids[:, 15]], tbl_16[ids[:, 16]], tbl_17[ids[:, 17]], tbl_18[ids[:, 18]], tbl_19[ids[:, 19]], tbl_20[ids[:, 20]], tbl_21[ids[:, 21]], tbl_22[ids[:, 22]], tbl_23[ids[:, 23]], tbl_24[ids[:, 24]], tbl_25[ids[:, 25]], tbl_26[ids[:, 26]], tbl_27[ids[:, 27]], tbl_28[ids[:, 28]], tbl_29[ids[:, 29]], tbl_30[ids[:, 30]], tbl_31[ids[:, 31]]], axis=1)
    z = _L0_rec_ref(e, L0_rec_W0, L0_rec_b0, L0_rec_W1, L0_rec_b1, L0_rec_W2, L0_rec_b2)
    z = z.reshape(z.shape[0], -1)
    h = jnp.concatenate([z, dense_ctx], axis=1)
    h = jnp.maximum(h @ W_top1 + b_top1, 0.0)
    h = jnp.maximum(h @ W_top2 + b_top2, 0.0)
    y = h @ W_top3
    return y

_drawn_inputs = setup_inputs


def setup_inputs(seed=0):
    import zlib

    import numpy as np

    out = dict(_drawn_inputs(seed))
    spreads = {'b_top1': (0.0, 0.356), 'b_top2': (0.0, 0.402)}
    factors = {'tbl_0': 8.0,
     'tbl_1': 8.0,
     'tbl_2': 8.0,
     'tbl_3': 8.0,
     'tbl_4': 8.0,
     'tbl_5': 8.0,
     'tbl_6': 8.0,
     'tbl_7': 8.0,
     'tbl_8': 8.0,
     'tbl_9': 8.0,
     'tbl_10': 8.0,
     'tbl_11': 8.0,
     'tbl_12': 8.0,
     'tbl_13': 8.0,
     'tbl_14': 8.0,
     'tbl_15': 8.0,
     'tbl_16': 8.0,
     'tbl_17': 8.0,
     'tbl_18': 8.0,
     'tbl_19': 8.0,
     'tbl_20': 8.0,
     'tbl_21': 8.0,
     'tbl_22': 8.0,
     'tbl_23': 8.0,
     'tbl_24': 8.0,
     'tbl_25': 8.0,
     'tbl_26': 8.0,
     'tbl_27': 8.0,
     'tbl_28': 8.0,
     'tbl_29': 8.0,
     'tbl_30': 8.0,
     'tbl_31': 8.0,
     'L0_rec_W0': 8.0,
     'L0_rec_W1': 8.0,
     'L0_rec_W2': 8.0,
     'L0_rec_b0': 4.936,
     'L0_rec_b1': 7.234,
     'L0_rec_b2': 7.274}
    for name, (base, spread) in spreads.items():
        noise = np.random.default_rng([zlib.crc32(name.encode()), seed]).standard_normal(out[name].shape)
        drawn = base * np.exp(spread * noise) if base else spread * noise
        out[name] = jnp.asarray(drawn.astype(out[name].dtype))
    for name, factor in factors.items():
        out[name] = (out[name] * factor).astype(out[name].dtype)
    return out
```

```python
from contextlib import ExitStack

import concourse.bass as bass
from concourse import mybir

ALU = mybir.AluOpType
ACT = mybir.ActivationFunctionType
F32 = mybir.dt.float32
I32 = mybir.dt.int32
U32 = mybir.dt.uint32

P = 128
FIELDS = 32
EMBED = 16
HALF = 64
QUAD = 4
COLS = QUAD * P
TILES_PER_BLOCK = EMBED // QUAD
GROUP = 4
CHUNKS = FIELDS * HALF // P
GROUPS = CHUNKS // GROUP
RING = 4
XROWS = FIELDS + FIELDS // 2
DENSE = 16
TOP1, TOP2 = 512, 256


def number(t):
    return TILES_PER_BLOCK * t[0] + t[1]


def after(t, n):
    return (t[0], t[1] + n)


def uses_of_parity(t):
    return TILES_PER_BLOCK // 2 * t[0] + t[1] // 2 + 1


PER_SLOT = 2 * GROUPS + 2


def entry0(t):
    first = isinstance(t[0], int) and number(t) == 0
    return 0 if first else PER_SLOT * number(t) - GROUPS


def entry1(t):
    return PER_SLOT * number(t) + 2


def entry2(t, tiles):
    last = isinstance(t[0], int) and number(t) == tiles - 1
    return PER_SLOT * number(t) + 2 * GROUPS - (2 if last else 0)


def ring(entry_of, k, *more):
    return entry_of((0, k), *more) % RING


def dlrm_tower(nc, dense_ctx, ids, tables, w_top1, b_top1, w_top2, b_top2, w_top3,
               w0, b0, w1, b1, w2, b2, xcols, out):
    batch = ids.shape[0]
    BLOCKS = batch // P
    TILES = BLOCKS * TILES_PER_BLOCK
    assert PER_SLOT * TILES_PER_BLOCK % RING == 0 and len(tables) == FIELDS

    with ExitStack() as ctx:
        def sb(name, shape, dt=F32):
            return ctx.enter_context(nc.sbuf_tensor(name, shape, dt))

        def ps(name, shape):
            return ctx.enter_context(nc.psum_tensor(name, shape, F32))

        def sem(name):
            return ctx.enter_context(nc.semaphore(name))

        w0T = sb("w0T", [P, GROUP, P])
        w0T_tail = sb("w0T_tail", [FIELDS, P])
        w1T = sb("w1T", [P, CHUNKS, P])
        w2T = sb("w2T", [P, CHUNKS, P])
        wt1 = sb("wt1", [P, 2, TOP1])
        wt1_dense = sb("wt1_dense", [DENSE, TOP1])
        wt2 = sb("wt2", [P, TOP1 // P, TOP2])
        wt3 = sb("wt3", [P, TOP2 // P])
        ident = sb("ident", [P, P])
        bias0 = sb("bias0", [P, 1])
        bias1 = sb("bias1", [P, 1])
        bias_sum = sb("bias_sum", [P, 2])
        neg_bias = sb("neg_bias", [P, 2])
        bias_all = sb("bias_all", [P, 2])
        bt1 = sb("bt1", [P, TOP1 // P])
        bt2 = sb("bt2", [P, TOP2 // P])
        ids_sb = sb("ids_sb", [P, BLOCKS, FIELDS], I32)
        ids_now = sb("ids_now", [P, FIELDS], I32)
        looked_up = sb("looked_up", [P, FIELDS, EMBED])
        emb = sb("emb", [P, EMBED, GROUP, FIELDS])
        xrows = sb("xrows", [XROWS, COLS])
        shifted = sb("shifted", [P, GROUP, COLS])
        shifted_tail = sb("shifted_tail", [FIELDS, COLS])
        spread = [sb(f"spread{p}", [P, CHUNKS, COLS]) for p in range(2)]
        prod = [sb(f"prod{r}", [P, GROUP, COLS]) for r in range(RING)]
        acc_kept = sb("acc_kept", [P, COLS])
        acc_last = sb("acc_last", [P, COLS])
        fold_kept = sb("fold_kept", [P, COLS // 2])
        fold_last = sb("fold_last", [P, COLS // 2])
        z_kept = sb("z_kept", [P, batch])
        z_last = sb("z_last", [P, batch])
        denseT = sb("denseT", [DENSE, batch])

        y0 = ps("y0", [P, COLS])
        y1 = ps("y1", [P, COLS])
        y2 = ps("y2", [P, COLS])
        h0 = ps("h0", [P, COLS])
        h1 = ps("h1", [P, COLS])
        xT = ps("xT", [P, COLS])
        prep = [ps(f"prep{n}", [P, GROUP, P]) for n in range(2)]

        s_ids = sem("s_ids")
        s_w0 = sem("s_w0")
        s_w1 = sem("s_w1")
        s_w2 = sem("s_w2")
        s_dense = sem("s_dense")
        s_biases = sem("s_biases")
        s_top_w = sem("s_top_w")
        s_ones = sem("s_ones")
        s_ident = sem("s_ident")
        s_neg = sem("s_neg")
        s_sym = sem("s_sym")
        s_turned = sem("s_turned")
        s_stored = sem("s_stored")
        s_now = sem("s_now")
        s_block = sem("s_block")
        s_looked = sem("s_looked")
        s_emb = sem("s_emb")
        s_xT = sem("s_xT")
        s_xrows = sem("s_xrows")
        s_xcols = sem("s_xcols")
        s_shifted = sem("s_shifted")
        s_spread = [[sem(f"s_spread{p}{g}") for g in range(GROUPS)] for p in range(2)]
        s_made = sem("s_made")
        s_used = sem("s_used")
        s_h0 = sem("s_h0")
        s_h1 = sem("s_h1")
        s_sum0 = sem("s_sum0")
        s_sum1 = sem("s_sum1")
        s_sum2 = sem("s_sum2")
        s_fold = sem("s_fold")
        s_z = sem("s_z")
        s_top = sem("s_top")
        s_relu = sem("s_relu")
        s_row = sem("s_row")
        s_out = sem("s_out")

        w0_raw = prod[0][:, 0:2, :].rearrange("p a b -> p (a b)")
        w0_wide = prod[1][:, :, :].rearrange("p a b -> p (a b)")
        w0_dist = spread[1][:, 0:2, :].rearrange("p a b -> p (a b)")
        w1_raw = prod[2][:, :, :].rearrange("p a b -> p (a b)")
        w2_raw = prod[3][:, :, :].rearrange("p a b -> p (a b)")
        dense_raw = spread[0][:, 0, 0:BLOCKS * DENSE]
        hidden1 = spread[0]
        hidden2 = spread[1]
        y_row = sb("y_row", [1, batch])

        PREP_GROUPS = 2 + 2 * GROUPS + 2

        block = ctx.enter_context(nc.Block())

        @block.sync
        def _(sp):
            sp.dma_start(ids_sb[:, :, :], ids.rearrange("(n p) f -> p n f", p=P)).then_inc(s_ids, 16)
            sp.dma_start(w0_raw, w0[:, :]).then_inc(s_w0, 16)
            sp.dma_start(w1_raw[0:HALF, :], w1[HALF:P, :]).then_inc(s_w1, 16)
            sp.dma_start(w1_raw[HALF:P, :], w1[0:HALF, :]).then_inc(s_w1, 16)
            sp.dma_start(w2_raw, w2[:, :]).then_inc(s_w2, 16)
            sp.dma_start(dense_raw.rearrange("p (n c) -> p n c", c=DENSE),
                         dense_ctx.rearrange("(n p) c -> p n c", p=P)).then_inc(s_dense, 16)
            for to, of in ((bias0[HALF:P, :], b0[HALF:P]), (bias1[0:HALF, :], b1[HALF:P]),
                           (bias_all[0:HALF, 0:1], b0[0:HALF]), (bias_all[HALF:P, 0:1], b1[0:HALF]),
                           (bias_all[:, 1:2], b2)):
                sp.dma_start(to, of.rearrange("(p a) -> p a", a=1)).then_inc(s_biases, 16)

            def load_factors(t):
                sp.wait_ge(s_xrows, number(t) + 1)
                sp.dma_start(xcols[number(t)], xrows[:, :]).then_inc(s_xcols, 16)
                sp.wait_ge(s_xcols, 16 * (number(t) + 1))
                x = xcols[number(t)]
                if not (isinstance(t[0], int) and number(t) == 0):
                    sp.wait_ge(s_made, entry0(after(t, -1)) + 2)
                for j in range(GROUP):
                    sp.dma_start(shifted[FIELDS * j:FIELDS * (j + 1), :, :],
                                 bass.AP(x.tensor, x.offset + j * COLS,
                                         [[COLS, FIELDS], [GROUP * COLS, GROUP], [1, COLS]])
                                 ).then_inc(s_shifted, 16)
                sp.dma_start(shifted_tail[:, :], x[FIELDS // 2:XROWS, :]).then_inc(s_shifted, 16)
                k = t[1]
                for g in range(GROUPS):
                    if not (isinstance(t[0], int) and number(t) < 2):
                        sp.wait_ge(s_made, entry2(after(t, -2), TILES) + g + 1)
                    for half in range(2):
                        sp.dma_start(spread[k % 2][HALF * half:HALF * (half + 1), GROUP * g:GROUP * (g + 1), :],
                                     bass.AP(x.tensor, x.offset + (2 * GROUP * g + half) * COLS,
                                             [[0, HALF], [2 * COLS, GROUP], [1, COLS]])
                                     ).then_inc(s_spread[k % 2][g], 16)

            sp.wait_ge(s_stored, PREP_GROUPS)
            load_factors((0, 0))
            load_factors((0, 1))
            sp.dma_start(wt1[:, :, :], w_top1[0:2 * P, :].rearrange("(c p) n -> p c n", p=P)).then_inc(s_top_w, 16)
            sp.dma_start(wt1_dense[:, :], w_top1[2 * P:2 * P + DENSE, :]).then_inc(s_top_w, 16)
            sp.dma_start(wt2[:, :, :], w_top2.rearrange("(c p) n -> p c n", p=P)).then_inc(s_top_w, 16)
            sp.dma_start(wt3[:, :], w_top3.rearrange("(c p) n -> p (c n)", p=P), allow_slow_non_contiguous=True).then_inc(s_top_w, 16)
            sp.dma_start(bt1[:, :], b_top1.rearrange("(c p) -> p c", p=P), allow_slow_non_contiguous=True).then_inc(s_top_w, 16)
            sp.dma_start(bt2[:, :], b_top2.rearrange("(c p) -> p c", p=P), allow_slow_non_contiguous=True).then_inc(s_top_w, 16)
            with sp.Fori(0, BLOCKS - 1) as i:
                for k in range(1, 1 + TILES_PER_BLOCK):
                    load_factors((i, k + 1))
            for k in range(1, TILES_PER_BLOCK - 1):
                load_factors((BLOCKS - 1, k + 1))
            for n in range(2):
                sp.wait_ge(s_row, n + 1)
                sp.dma_start(out.rearrange("b a -> a b")[:, TOP1 * n:TOP1 * (n + 1)],
                             y_row[:, TOP1 * n:TOP1 * (n + 1)]).then_inc(s_out, 16)
            sp.wait_ge(s_out, 32)

        @block.gpsimd
        def _(pool):
            pool.memset(ident[:, :], 0.0).then_inc(s_ones, 1)
            pool.wait_ge(s_ones, 1)
            pool.affine_select(out=ident[:, :], in_=ident[:, :], compare_op=ALU.not_equal, fill=1.0,
                               base=0, pattern=[[-1, P]], channel_multiplier=1).then_inc(s_ident, 1)
            pool.wait_ge(s_ids, 16)

            def look_up(b):
                pool.tensor_copy(ids_now[:, :], ids_sb[:, bass.ds(b, 1), :]).then_inc(s_now, 1)
                pool.wait_ge(s_now, b + 1)
                pool.sem_inc(s_block, 1)
                for f in range(FIELDS):
                    pool.indirect_dma_start(
                        out=looked_up[:, f, :], out_offset=None, in_=tables[f][:, :],
                        in_offset=bass.IndirectOffsetOnAxis(ap=ids_now[:, f:f + 1].bitcast(U32), axis=0),
                    ).then_inc(s_looked, 16)

            look_up(0)
            with pool.Fori(1, BLOCKS) as b:
                pool.wait_ge(s_looked, 16 * FIELDS * b)
                pool.wait_ge(s_emb, b)
                look_up(b)

        @block.tensor
        def _(pe):
            def turn(n, chunks, rows, source):
                if n >= 2:
                    pe.wait_ge(s_stored, n - 1)
                for c in range(chunks):
                    last = pe.transpose(prep[n % 2][0:rows, c, :], source(c), ident[:, :])
                last.then_inc(s_turned, 1)

            pe.wait_ge(s_ident, 1)
            pe.wait_ge(s_sym, 6)
            turn(0, GROUP, P, lambda c: w0_dist[:, P * c:P * (c + 1)])
            turn(1, 1, FIELDS, lambda c: w0_dist[:, P * GROUP:P * GROUP + FIELDS])
            pe.wait_ge(s_w1, 32)
            for g in range(GROUPS):
                turn(2 + g, GROUP, P, lambda c: w1_raw[:, P * (GROUP * g + c):P * (GROUP * g + c + 1)])
            pe.wait_ge(s_w2, 16)
            for g in range(GROUPS):
                turn(2 + GROUPS + g, GROUP, P, lambda c: w2_raw[:, P * (GROUP * g + c):P * (GROUP * g + c + 1)])
            pe.wait_ge(s_dense, 16)
            for g in range(2):
                turn(2 + 2 * GROUPS + g, GROUP, DENSE,
                     lambda c: dense_raw[:, DENSE * (GROUP * g + c):DENSE * (GROUP * g + c + 1)])
            pe.wait_ge(s_stored, PREP_GROUPS)

            def turn_x(t):
                q = t[1] % TILES_PER_BLOCK
                if q == 0:
                    pe.wait_ge(s_emb, t[0] + t[1] // TILES_PER_BLOCK + 1)
                if not (isinstance(t[0], int) and number(t) == 0):
                    pe.wait_ge(s_xrows, number(t))
                    pe.wait_ge(s_made, entry0(after(t, -1)) + 2)
                for e in range(QUAD):
                    last = pe.transpose(xT[:, P * e:P * (e + 1)],
                                        emb[:, QUAD * q + e, :, :].rearrange("p a f -> p (a f)"), ident[:, :])
                last.then_inc(s_xT, 1)

            def layer0(t):
                pe.wait_ge(s_h0, number(t))
                pe.wait_ge(s_sum0, number(t))
                e, r = entry0(t), ring(entry0, t[1])
                pe.wait_ge(s_made, e + 1)
                for c in range(GROUP):
                    last = pe.matmul(y0[:, :], w0T[:, c, :], prod[r][:, c, :], start=(c == 0), stop=False)
                last.then_inc(s_used, 1)
                pe.wait_ge(s_made, e + 2)
                pe.matmul(y0[:, :], w0T_tail[:, :], prod[(r + 1) % RING][0:FIELDS, 0, :],
                          start=False, stop=True).then_inc(s_used, 1)

            def big_layer(y, w, e, r, between=None):
                for g in range(GROUPS):
                    pe.wait_ge(s_made, e + g + 1)
                    for c in range(GROUP):
                        last = pe.matmul(y[:, :], w[:, GROUP * g + c, :], prod[(r + g) % RING][:, c, :],
                                         start=(g == 0 and c == 0), stop=(g == GROUPS - 1 and c == GROUP - 1))
                    last.then_inc(s_used, 1)
                    if g == 0 and between:
                        between()

            def layer1(t):
                pe.wait_ge(s_h1, number(t))
                pe.wait_ge(s_sum1, number(t))
                big_layer(y1, w1T, entry1(t), ring(entry1, t[1]))

            def layer2(t, between=None):
                pe.wait_ge(s_sum2, number(t))
                big_layer(y2, w2T, entry2(t, TILES),
                          entry2(t, TILES) % RING if isinstance(t[0], int) else ring(entry2, t[1], TILES),
                          between)

            def slot(s):
                layer2(after(s, -1), lambda: turn_x(after(s, 1)))
                layer1(s)
                layer0(after(s, 1))

            turn_x((0, 0))
            layer0((0, 0))
            turn_x((0, 1))
            layer1((0, 0))
            layer0((0, 1))
            with pe.Fori(0, BLOCKS - 1) as i:
                for k in range(1, 1 + TILES_PER_BLOCK):
                    slot((i, k))
            for k in range(1, TILES_PER_BLOCK - 1):
                slot((BLOCKS - 1, k))
            last_tile = (BLOCKS - 1, TILES_PER_BLOCK - 1)
            layer2(after(last_tile, -1))
            layer1(last_tile)
            layer2(last_tile)

            banks = [y0, y1, h0, h1, xT, y2]
            pe.wait_ge(s_z, 2 * BLOCKS)
            pe.wait_ge(s_top_w, 6 * 16)
            step = 0
            for n in range(2):
                rows = slice(TOP1 * n, TOP1 * (n + 1))
                for m in range(TOP1 // P):
                    if step >= len(banks):
                        pe.wait_ge(s_relu, step - len(banks) + 1)
                    bank = banks[step % len(banks)]
                    cols = slice(P * m, P * (m + 1))
                    pe.matmul(bank[:, :], wt1[:, 0, cols], z_kept[:, rows], start=True, stop=False)
                    pe.matmul(bank[:, :], wt1[:, 1, cols], z_last[:, rows], start=False, stop=False)
                    pe.matmul(bank[:, :], wt1_dense[:, cols], denseT[:, rows],
                              start=False, stop=True).then_inc(s_top, 1)
                    step += 1
            for n in range(2):
                pe.wait_ge(s_relu, TOP1 // P * (n + 1))
                for m in range(TOP2 // P):
                    pe.wait_ge(s_relu, step - len(banks) + 1)
                    bank = banks[step % len(banks)]
                    for c in range(TOP1 // P):
                        last = pe.matmul(bank[:, :], wt2[:, c, P * m:P * (m + 1)],
                                         hidden1[:, TOP1 // P * n + c, :], start=(c == 0), stop=(c == TOP1 // P - 1))
                    last.then_inc(s_top, 1)
                    step += 1
            for n in range(2):
                pe.wait_ge(s_relu, 2 * TOP1 // P + TOP2 // P * (n + 1))
                for c in range(TOP2 // P):
                    last = pe.matmul(prep[n].rearrange("p a b -> p (a b)")[0:1, :], wt3[:, c:c + 1],
                                     hidden2[:, TOP2 // P * n + c, :], start=(c == 0), stop=(c == TOP2 // P - 1))
                last.then_inc(s_top, 1)

        @block.scalar
        def _(act):
            act.wait_ge(s_biases, 5 * 16)

            def take_rows(t):
                b = t[0] + t[1] // TILES_PER_BLOCK
                act.wait_ge(s_looked, 16 * FIELDS * (b + 1))
                act.wait_ge(s_xT, number(t))
                act.copy(emb[:, :, :, :], looked_up.rearrange("p f e -> p e f").unsqueeze(2).to_broadcast(
                    [P, EMBED, GROUP, FIELDS])).then_inc(s_emb, 1)

            def take_x(t):
                act.wait_ge(s_xT, number(t) + 1)
                act.wait_ge(s_xcols, 16 * number(t))
                act.copy(xrows[:, :], xT[0:XROWS, :]).then_inc(s_xrows, 1)

            def go_on(h, y, half, bias, s_h):
                lanes = slice(half * HALF, half * HALF + HALF)
                for to in (slice(0, HALF), slice(HALF, P)):
                    last = act.activation(h[to, :], y[lanes, :], ACT.Relu, bias=bias[lanes, :])
                last.then_inc(s_h, 1)

            def slot(s):
                nxt = after(s, 1)
                if nxt[1] % TILES_PER_BLOCK == 0:
                    take_rows(nxt)
                take_x(nxt)
                act.wait_ge(s_used, entry1(s) + GROUPS)
                go_on(h1, y1, 0, bias1, s_h1)
                act.wait_ge(s_used, entry0(nxt) + 2)
                go_on(h0, y0, 1, bias0, s_h0)

            take_rows((0, 0))
            take_x((0, 0))
            act.wait_ge(s_used, 2)
            go_on(h0, y0, 1, bias0, s_h0)
            slot((0, 0))
            with act.Fori(0, BLOCKS - 1) as i:
                for k in range(1, 1 + TILES_PER_BLOCK):
                    slot((i, k))
            for k in range(1, TILES_PER_BLOCK - 1):
                slot((BLOCKS - 1, k))
            last_tile = (BLOCKS - 1, TILES_PER_BLOCK - 1)
            act.wait_ge(s_used, entry1(last_tile) + GROUPS)
            go_on(h1, y1, 0, bias1, s_h1)

            banks = [y0, y1, h0, h1, xT, y2]
            act.wait_ge(s_top_w, 6 * 16)
            step = 0
            for n in range(2):
                for m in range(TOP1 // P):
                    act.wait_ge(s_top, step + 1)
                    act.activation(hidden1[:, TOP1 // P * n + m, :], banks[step % len(banks)][:, :], ACT.Relu,
                                   bias=bt1[:, m:m + 1]).then_inc(s_relu, 1)
                    step += 1
            for n in range(2):
                for m in range(TOP2 // P):
                    act.wait_ge(s_top, step + 1)
                    act.activation(hidden2[:, TOP2 // P * n + m, :], banks[step % len(banks)][:, :], ACT.Relu,
                                   bias=bt2[:, m:m + 1]).then_inc(s_relu, 1)
                    step += 1
            for n in range(2):
                act.wait_ge(s_top, step + 1)
                act.copy(y_row[:, TOP1 * n:TOP1 * (n + 1)],
                         prep[n].rearrange("p a b -> p (a b)")[0:1, :]).then_inc(s_row, 1)
                step += 1

        @block.vector
        def _(dve):
            wide = w0_wide.rearrange("p (f g) -> p f g", g=2 * FIELDS)
            raw = w0_raw.rearrange("p (f g) -> p f g", g=FIELDS)
            dve.wait_ge(s_w0, 16)
            for n in range(2):
                dve.tensor_tensor(wide[:, :, FIELDS * n:FIELDS * (n + 1)], raw, raw.rearrange("p f g -> p g f"),
                                  ALU.add).then_inc(s_sym, 1)
            dve.wait_ge(s_sym, 2)

            def diagonal(ap, width, start, count):
                return bass.AP(ap.tensor, ap.offset + start, [list(ap.ap[0]), [width + 1, count]])

            H = FIELDS // 2
            dve.tensor_copy(w0_dist[:, FIELDS:FIELDS * H].rearrange("p (d f) -> p d f", f=FIELDS),
                            bass.AP(w0_wide.tensor, w0_wide.offset + 1,
                                    [list(w0_wide.ap[0]), [1, H - 1], [2 * FIELDS + 1, FIELDS]])).then_inc(s_sym, 1)
            dve.tensor_copy(w0_dist[:, 0:FIELDS], diagonal(w0_raw, FIELDS, 0, FIELDS)).then_inc(s_sym, 1)
            dve.tensor_copy(w0_dist[:, FIELDS * H:FIELDS * H + H],
                            diagonal(w0_raw, FIELDS, H, H)).then_inc(s_sym, 1)
            dve.tensor_copy(w0_dist[:, FIELDS * H + H:FIELDS * (H + 1)],
                            diagonal(w0_raw, FIELDS, H * FIELDS, H)).then_inc(s_sym, 1)
            homes = [w0T[:, :, :], w0T_tail[:, :]]
            homes += [w1T[:, GROUP * g:GROUP * (g + 1), :] for g in range(GROUPS)]
            homes += [w2T[:, GROUP * g:GROUP * (g + 1), :] for g in range(GROUPS)]
            homes += [denseT[:, TOP1 * g:TOP1 * (g + 1)] for g in range(2)]
            for n, home in enumerate(homes):
                dve.wait_ge(s_turned, n + 1)
                if n == 1:
                    source = prep[1][0:FIELDS, 0, :]
                elif n >= 2 + 2 * GROUPS:
                    source = prep[n % 2][0:DENSE, :, :].rearrange("p a b -> p (a b)")
                else:
                    source = prep[n % 2][:, :, :]
                dve.tensor_copy(home, source).then_inc(s_stored, 1)
            dve.wait_ge(s_biases, 5 * 16)
            dve.tensor_scalar(neg_bias[:, :], bias_all[:, :], -1.0, None, ALU.mult).then_inc(s_neg, 1)
            dve.tensor_scalar(bias_sum[:, :], bias_all[:, :], float(EMBED), None, ALU.mult).then_inc(s_neg, 1)
            dve.wait_ge(s_neg, 2)
            dve.wait_ge(s_stored, PREP_GROUPS)

            def multiply(e, r, chunks, a, b, lanes=P):
                if not isinstance(e, int) or e >= RING:
                    dve.wait_ge(s_used, e - RING + 1)
                dve.tensor_tensor(prod[r % RING][0:lanes, 0:chunks, :], a,
                                  b.unsqueeze(1).to_broadcast([lanes, chunks, COLS]), ALU.mult).then_inc(s_made, 1)

            def add_up(acc, y, lanes, col, t, s_sum):
                if t[1] % TILES_PER_BLOCK == 0:
                    dve.tensor_scalar(acc[lanes, :], y[lanes, :], neg_bias[lanes, col:col + 1], None,
                                      ALU.max).then_inc(s_sum, 1)
                else:
                    dve.wait_ge(s_sum, number(t))
                    dve.scalar_tensor_tensor(out=acc[lanes, :], in0=y[lanes, :],
                                             scalar=neg_bias[lanes, col:col + 1], in1=acc[lanes, :],
                                             op0=ALU.max, op1=ALU.add).then_inc(s_sum, 1)

            def fold(acc, half, z, col, t, s_sum):
                b = t[0] + t[1] // TILES_PER_BLOCK
                dve.wait_ge(s_sum, number(t) + 1)
                dve.tensor_tensor(half[:, :], acc[:, 0:COLS // 2], acc[:, COLS // 2:COLS],
                                  ALU.add).then_inc(s_fold, 1)
                dve.wait_ge(s_fold, 2 * b + col + 1)
                dve.scalar_tensor_tensor(out=z[:, bass.ds(P * b, P)], in0=half[:, 0:P],
                                         scalar=bias_sum[:, col:col + 1], in1=half[:, P:2 * P],
                                         op0=ALU.add, op1=ALU.add).then_inc(s_z, 1)

            KEPT0, KEPT1, ALL = slice(0, HALF), slice(HALF, P), slice(0, P)

            def sum0(t):
                dve.wait_ge(s_used, entry0(t) + 2)
                add_up(acc_kept, y0, KEPT0, 0, t, s_sum0)

            def sum1(t):
                dve.wait_ge(s_used, entry1(t) + GROUPS)
                add_up(acc_kept, y1, KEPT1, 0, t, s_sum1)
                if t[1] % TILES_PER_BLOCK == TILES_PER_BLOCK - 1:
                    dve.wait_ge(s_sum0, number(t) + 1)
                    fold(acc_kept, fold_kept, z_kept, 0, t, s_sum1)

            def sum2(t):
                dve.wait_ge(s_used, entry2(t, TILES) + GROUPS)
                add_up(acc_last, y2, ALL, 1, t, s_sum2)
                if t[1] % TILES_PER_BLOCK == TILES_PER_BLOCK - 1:
                    fold(acc_last, fold_last, z_last, 1, t, s_sum2)

            def group(buffer, g):
                return buffer[:, GROUP * g:GROUP * (g + 1), :]

            def layer0(t):
                dve.wait_ge(s_shifted, 16 * (GROUP + 1) * (number(t) + 1))
                dve.wait_ge(s_xT, number(t) + 1)
                e, r = entry0(t), ring(entry0, t[1])
                multiply(e, r, GROUP, shifted[:, :, :], xT[:, :])
                multiply(e + 1, r + 1, 1, shifted_tail[:, :].unsqueeze(1), xT[0:FIELDS, :], FIELDS)

            def layer1(t):
                dve.wait_ge(s_h0, number(t) + 1)
                e, r, p = entry1(t), ring(entry1, t[1]), t[1] % 2
                for g in range(GROUPS):
                    dve.wait_ge(s_spread[p][g], 32 * uses_of_parity(t))
                    multiply(e + g, r + g, GROUP, group(spread[p], g), h0[:, :])

            def layer2(t, between=None):
                dve.wait_ge(s_h1, number(t) + 1)
                e = entry2(t, TILES)
                r = e % RING if isinstance(t[0], int) else ring(entry2, t[1], TILES)
                for g in range(GROUPS):
                    multiply(e + g, r + g, GROUP, group(spread[t[1] % 2], g), h1[:, :])
                    if g == 1:
                        sum1(t)

            def slot(s):
                layer2(after(s, -1))
                sum0(s)
                layer1(s)
                layer0(after(s, 1))
                sum2(after(s, -1))

            layer0((0, 0))
            sum0((0, 0))
            layer1((0, 0))
            layer0((0, 1))
            with dve.Fori(0, BLOCKS - 1) as i:
                for k in range(1, 1 + TILES_PER_BLOCK):
                    slot((i, k))
            for k in range(1, TILES_PER_BLOCK - 1):
                slot((BLOCKS - 1, k))
            last_tile = (BLOCKS - 1, TILES_PER_BLOCK - 1)
            layer2(after(last_tile, -1))
            sum0(last_tile)
            layer1(last_tile)
            sum2(after(last_tile, -1))
            layer2(last_tile)
            sum2(last_tile)


TABLES = FIELDS


def kernel(**inputs):
    import numpy as np
    import concourse.bacc as bacc
    from concourse.bass_utils import run_bass_kernel_spmd

    nc = bacc.Bacc("TRN2", target_bir_lowering=False, num_devices=1)
    arrays = {}

    def dram(name):
        a = np.ascontiguousarray(inputs[name])
        arrays["in_" + name] = a
        return nc.dram_tensor("in_" + name, a.shape, mybir.dt.from_np(a.dtype), kind="ExternalInput").ap()

    batch = inputs["ids"].shape[0]
    tiles = batch // P * TILES_PER_BLOCK
    tables = [dram(f"tbl_{f}") for f in range(TABLES)]
    xcols = nc.dram_tensor("xcols", (tiles, XROWS, COLS), F32, kind="Internal").ap()
    out = nc.dram_tensor("out", (batch, 1), F32, kind="ExternalOutput").ap()
    dlrm_tower(nc, dram("dense_ctx"), dram("ids"), tables, dram("W_top1"), dram("b_top1"),
               dram("W_top2"), dram("b_top2"), dram("W_top3"), dram("L0_rec_W0"), dram("L0_rec_b0"),
               dram("L0_rec_W1"), dram("L0_rec_b1"), dram("L0_rec_W2"), dram("L0_rec_b2"), xcols, out)
    result = run_bass_kernel_spmd(nc, [arrays], core_ids=[0])
    return result.results[0]["out"]
```

```python
from contextlib import ExitStack

import concourse.bass as bass
from concourse import mybir

ALU = mybir.AluOpType
ACT = mybir.ActivationFunctionType
F32 = mybir.dt.float32
F32R = mybir.dt.float32r
I32 = mybir.dt.int32
U32 = mybir.dt.uint32

P = 128
FIELDS = 32
EMBED = 16
HALF = 64
QUAD = 4
COLS = QUAD * P
TILES_PER_BLOCK = EMBED // QUAD
ITEM = 2
GROUP = 4
CHUNKS = FIELDS * HALF // P
GROUPS = CHUNKS // GROUP
ITEMS = CHUNKS // ITEM
XROWS = FIELDS + FIELDS // 2
DENSE = 16
TOP1, TOP2 = 512, 256


def number(t):
    return TILES_PER_BLOCK * t[0] + t[1]


def after(t, n):
    return (t[0], t[1] + n)


def uses_of_parity(t):
    return TILES_PER_BLOCK // 2 * t[0] + t[1] // 2 + 1


TAIL = (0, -1)
SLOT = [(1, 0), (1, 1), (2, 0), (1, 2), (2, 1), (1, 3), (0, 0), (2, 2), TAIL, (1, 4), (0, 1),
        (2, 3), (1, 5), (2, 4), (1, 6), (2, 5), (1, 7), (2, 6), (2, 7)]
START = 2

WHOLE, BY_POOL, BY_DVE = range(3)
SPLIT = (BY_POOL, BY_DVE)
RING = (4, 4, 2)
RAW_RING = (None, 2, 1)


LOOKUPS_AFTER = (0, 1, 2, 1, 1, 2, 1)


def kind_of(item):
    if item[0] == 1:
        return WHOLE
    return BY_DVE if item[0] == 0 or item == (2, 6) else BY_POOL


def slot_items(n, tiles):
    tile = {0: n + 1, 1: n, 2: n - 1}
    return [x for x in SLOT if 0 <= tile[x[0]] < tiles]


def of_kind(items, kind):
    return [x for x in items if x != TAIL and kind_of(x) == kind]


class Plan:

    def __init__(self, tiles):
        self.tiles = tiles
        self.steady = [len(of_kind(SLOT, kind)) for kind in (WHOLE, *SPLIT)]
        assert all(TILES_PER_BLOCK * n % ring == 0 for n, ring in zip(self.steady, RING))
        assert all(TILES_PER_BLOCK * self.steady[kind] % RAW_RING[kind] == 0 for kind in SPLIT)

    def items(self, s):
        return slot_items(number(s), self.tiles) if isinstance(s[0], int) else SLOT

    def before(self, kind, n):
        return sum(len(of_kind(slot_items(m, self.tiles), kind)) for m in range(-1, n))

    def entry(self, s, item):
        kind = kind_of(item)
        rank = of_kind(self.items(s), kind).index(item)
        if isinstance(s[0], int):
            return self.before(kind, number(s)) + rank
        return TILES_PER_BLOCK * self.steady[kind] * s[0] + self.before(kind, s[1]) + rank

    def place(self, s, item, ring):
        kind = kind_of(item)
        if isinstance(s[0], int):
            return self.entry(s, item) % ring[kind]
        return (self.before(kind, s[1]) + of_kind(SLOT, kind).index(item)) % ring[kind]


def dlrm_tower(nc, dense_ctx, ids, tables, w_top1, b_top1, w_top2, b_top2, w_top3,
               w0, b0, w1, b1, w2, b2, xcols, out):
    batch = ids.shape[0]
    BLOCKS = batch // P
    TILES = BLOCKS * TILES_PER_BLOCK
    assert len(tables) == FIELDS
    plan = Plan(TILES)
    LAST0, LAST1, LAST2 = (0, GROUP // ITEM - 1), (1, ITEMS - 1), (2, ITEMS - 1)

    with ExitStack() as ctx:
        def sb(name, shape, dt=F32):
            return ctx.enter_context(nc.sbuf_tensor(name, shape, dt))

        def ps(name, shape):
            return ctx.enter_context(nc.psum_tensor(name, shape, F32))

        def sem(name):
            return ctx.enter_context(nc.semaphore(name))

        w0T_high = sb("w0T_high", [P, GROUP, P], F32R)
        w0T_low = sb("w0T_low", [P, GROUP, P], F32R)
        w0T_tail = sb("w0T_tail", [P, P], F32R)
        w1T = sb("w1T", [P, CHUNKS, P])
        w2T_high = sb("w2T_high", [P, CHUNKS, P], F32R)
        w2T_low = sb("w2T_low", [P, CHUNKS, P], F32R)
        wt3 = sb("wt3", [P, TOP2 // P])
        ident = sb("ident", [P, P])
        bias0 = sb("bias0", [P, 1])
        bias1 = sb("bias1", [P, 1])
        bias_sum = sb("bias_sum", [P, 2])
        neg_bias = sb("neg_bias", [P, 2])
        bias_all = sb("bias_all", [P, 2])
        bt1 = sb("bt1", [P, TOP1 // P])
        bt2 = sb("bt2", [P, TOP2 // P])
        ids_sb = sb("ids_sb", [P, BLOCKS, FIELDS], I32)
        ids_now = sb("ids_now", [P, FIELDS], I32)
        looked_up = sb("looked_up", [P, FIELDS, EMBED])
        emb = sb("emb", [P, FIELDS, EMBED])
        four_times = sb("four_times", [P, QUAD, GROUP, FIELDS])
        xrows = sb("xrows", [XROWS, COLS])
        shifted = sb("shifted", [P, GROUP, COLS])
        shifted_tail = sb("shifted_tail", [P, COLS])
        spread = [sb(f"spread{p}", [P, CHUNKS, COLS]) for p in range(2)]
        prod = [sb(f"prod{r}", [P, ITEM, COLS]) for r in range(RING[WHOLE])]
        tail = sb("tail", [P, COLS])
        tail_high = sb("tail_high", [P, COLS], F32R)
        tail_parts = sb("tail_parts", [P, COLS], F32R)
        unsplit = [None] + [[sb(f"unsplit{kind}{r}", [P, ITEM, COLS]) for r in range(RAW_RING[kind])]
                            for kind in SPLIT]
        high = [None] + [[sb(f"high{kind}{r}", [P, ITEM, COLS], F32R) for r in range(RING[kind])]
                         for kind in SPLIT]
        low = [None] + [[sb(f"low{kind}{r}", [P, ITEM, COLS], F32R) for r in range(RING[kind])]
                        for kind in SPLIT]
        acc_kept = sb("acc_kept", [P, COLS])
        acc_last = sb("acc_last", [P, COLS])
        z_kept = sb("z_kept", [P, batch])
        z_last = sb("z_last", [P, batch])

        y0 = ps("y0", [P, COLS])
        y1 = ps("y1", [P, COLS])
        y2 = [ps(f"y2_{p}", [P, COLS]) for p in range(2)]
        h0 = [ps(f"h0_{p}", [P, COLS]) for p in range(2)]
        h1 = ps("h1", [P, COLS])
        xT = ps("xT", [P, COLS])
        prep = [bank[:, :].rearrange("p (a b) -> p a b", b=P) for bank in y2]

        s_ids = sem("s_ids")
        s_w0 = sem("s_w0")
        s_w1 = sem("s_w1")
        s_w2 = sem("s_w2")
        s_dense = sem("s_dense")
        s_biases = sem("s_biases")
        s_top_w = sem("s_top_w")
        s_top_b = sem("s_top_b")
        s_ones = sem("s_ones")
        s_zero = sem("s_zero")
        s_ident = sem("s_ident")
        s_neg = sem("s_neg")
        s_sym = sem("s_sym")
        s_turned = sem("s_turned")
        s_stored = sem("s_stored")
        s_w_high = sem("s_w_high")
        s_tail_w = sem("s_tail_w")
        s_denseT = sem("s_denseT")
        s_now = sem("s_now")
        s_block = sem("s_block")
        s_looked = sem("s_looked")
        s_emb = sem("s_emb")
        s_four = sem("s_four")
        s_xT = sem("s_xT")
        s_xrows = sem("s_xrows")
        s_xcols = sem("s_xcols")
        s_shifted = sem("s_shifted")
        s_shifted_tail = sem("s_shifted_tail")
        s_spread = [[sem(f"s_spread{p}{g}") for g in range(GROUPS)] for p in range(2)]
        s_made = [sem(f"s_made{kind}") for kind in (WHOLE, *SPLIT)]
        s_high = [None] + [sem(f"s_high{kind}") for kind in SPLIT]
        s_low = [None] + [sem(f"s_low{kind}") for kind in SPLIT]
        s_used = [sem(f"s_used{kind}") for kind in (WHOLE, *SPLIT)]
        s_tail = sem("s_tail")
        s_tail_high = sem("s_tail_high")
        s_tail_low = sem("s_tail_low")
        s_tail_used = sem("s_tail_used")
        s_h0 = sem("s_h0")
        s_h1 = sem("s_h1")
        s_sum0 = sem("s_sum0")
        s_sum1 = sem("s_sum1")
        s_sum2 = sem("s_sum2")
        s_fold = sem("s_fold")
        s_z = sem("s_z")
        s_top = sem("s_top")
        s_relu = sem("s_relu")
        s_row = sem("s_row")
        s_out = sem("s_out")

        flat = lambda ap: ap.rearrange("p a b -> p (a b)")
        w1_raw = flat(spread[0][:, 0:4, :])
        w2_raw = flat(spread[0][:, 4:8, :])
        w0_raw = flat(spread[0][:, 8:10, :])
        w0_wide = flat(spread[0][:, 10:14, :])
        w0_dist = flat(spread[0][:, 14:16, :])
        hidden1 = spread[0][:, 0:8, :]
        wt1 = spread[0][:, 8:10, :]
        wt2 = flat(spread[0][:, 10:12, :]).rearrange("p (c n) -> p c n", n=TOP2)
        wt1_dense = spread[0][0:DENSE, 12, :]
        denseT = flat(spread[0][0:DENSE, 13:15, :])
        dense_raw = spread[0][:, 15, 0:BLOCKS * DENSE]
        hidden2 = spread[1]
        y_rows = [acc_kept, acc_last]

        PREP_GROUPS = 2 + 2 * GROUPS

        block = ctx.enter_context(nc.Block())

        @block.sync
        def _(sp):
            sp.dma_start(ids_sb[:, :, :], ids.rearrange("(n p) f -> p n f", p=P)).then_inc(s_ids, 16)
            sp.dma_start(w0_raw, w0[:, :]).then_inc(s_w0, 16)
            sp.dma_start(w1_raw[0:HALF, :], w1[HALF:P, :]).then_inc(s_w1, 16)
            sp.dma_start(w1_raw[HALF:P, :], w1[0:HALF, :]).then_inc(s_w1, 16)
            sp.dma_start(w2_raw, w2[:, :]).then_inc(s_w2, 16)
            for to, of in ((bias0[HALF:P, :], b0[HALF:P]), (bias1[0:HALF, :], b1[HALF:P]),
                           (bias_all[0:HALF, 0:1], b0[0:HALF]), (bias_all[HALF:P, 0:1], b1[0:HALF]),
                           (bias_all[:, 1:2], b2)):
                sp.dma_start(to, of.rearrange("(p a) -> p a", a=1)).then_inc(s_biases, 16)

            def load_factors(t):
                sp.wait_ge(s_xrows, number(t) + 1)
                sp.dma_start(xcols[number(t)], xrows[:, :]).then_inc(s_xcols, 16)
                sp.wait_ge(s_xcols, 16 * (number(t) + 1))
                x = xcols[number(t)]
                for j in range(GROUP):
                    sp.dma_start(shifted[FIELDS * j:FIELDS * (j + 1), :, :],
                                 bass.AP(x.tensor, x.offset + j * COLS,
                                         [[COLS, FIELDS], [GROUP * COLS, GROUP], [1, COLS]])
                                 ).then_inc(s_shifted, 16)
                for j in range(GROUP):
                    sp.dma_start(shifted_tail[FIELDS * j:FIELDS * (j + 1), :],
                                 x[FIELDS // 2:XROWS, :]).then_inc(s_shifted_tail, 16)
                k = t[1]
                for g in range(GROUPS):
                    if not (isinstance(t[0], int) and number(t) < 2):
                        item = (2, GROUP // ITEM * (g + 1) - 1)
                        sp.wait_ge(s_made[kind_of(item)], plan.entry(after(t, -1), item) + 1)
                    for half in range(2):
                        sp.dma_start(spread[k % 2][HALF * half:HALF * (half + 1), GROUP * g:GROUP * (g + 1), :],
                                     bass.AP(x.tensor, x.offset + (2 * GROUP * g + half) * COLS,
                                             [[0, HALF], [2 * COLS, GROUP], [1, COLS]])
                                     ).then_inc(s_spread[k % 2][g], 16)

            sp.dma_start(wt3[:, :], w_top3.rearrange("(c p) n -> p (c n)", p=P), allow_slow_non_contiguous=True).then_inc(s_top_b, 16)
            sp.dma_start(bt1[:, :], b_top1.rearrange("(c p) -> p c", p=P), allow_slow_non_contiguous=True).then_inc(s_top_b, 16)
            sp.dma_start(bt2[:, :], b_top2.rearrange("(c p) -> p c", p=P), allow_slow_non_contiguous=True).then_inc(s_top_b, 16)
            sp.wait_ge(s_stored, PREP_GROUPS)
            load_factors((0, 0))
            load_factors((0, 1))
            load_factors((0, 2))
            with sp.Fori(0, BLOCKS - 1) as i:
                for k in range(START, START + TILES_PER_BLOCK):
                    load_factors((i, k + 1))
            load_factors((BLOCKS - 1, START + 1))
            sp.wait_ge(s_made[kind_of(LAST2)], plan.entry((BLOCKS - 1, TILES_PER_BLOCK - 1), LAST2) + 1)
            sp.dma_start(dense_raw.rearrange("p (n c) -> p n c", c=DENSE),
                         dense_ctx.rearrange("(n p) c -> p n c", p=P)).then_inc(s_dense, 16)
            sp.dma_start(wt1, w_top1[0:2 * P, :].rearrange("(c p) n -> p c n", p=P)).then_inc(s_top_w, 16)
            sp.dma_start(wt1_dense, w_top1[2 * P:2 * P + DENSE, :]).then_inc(s_top_w, 16)
            sp.dma_start(wt2, w_top2.rearrange("(c p) n -> p c n", p=P)).then_inc(s_top_w, 16)
            for n in range(2):
                sp.wait_ge(s_row, n + 1)
                sp.dma_start(out.rearrange("b a -> a b")[:, TOP1 * n:TOP1 * (n + 1)],
                             y_rows[n][0:1, :]).then_inc(s_out, 16)
            sp.wait_ge(s_out, 32)

        @block.gpsimd
        def _(pool):
            pool.memset(ident[:, :], 0.0).then_inc(s_ones, 1)
            pool.wait_ge(s_ones, 1)
            pool.affine_select(out=ident[:, :], in_=ident[:, :], compare_op=ALU.not_equal, fill=1.0,
                               base=0, pattern=[[-1, P]], channel_multiplier=1).then_inc(s_ident, 1)
            pool.memset(tail_high[:, :].bitcast(F32), 0.0).then_inc(s_zero, 1)
            pool.wait_ge(s_ids, 16)

            def next_ids(b):
                pool.tensor_copy(ids_now[:, :], ids_sb[:, bass.ds(b, 1), :]).then_inc(s_now, 1)
                pool.wait_ge(s_now, b + 1)
                pool.sem_inc(s_block, 1)

            def begin(b):
                pool.wait_ge(s_looked, 16 * FIELDS * b)
                pool.wait_ge(s_emb, b)
                next_ids(b)

            def look_up(f):
                pool.indirect_dma_start(
                    out=looked_up[:, f, :], out_offset=None, in_=tables[f][:, :],
                    in_offset=bass.IndirectOffsetOnAxis(ap=ids_now[:, f:f + 1].bitcast(U32), axis=0),
                ).then_inc(s_looked, 16)

            def split_low(s, item):
                e, kind = plan.entry(s, item), BY_POOL
                pool.wait_ge(s_high[kind], e + 1)
                r = plan.place(s, item, RING)
                pool.tensor_tensor(low[kind][r][:, :, :], unsplit[kind][plan.place(s, item, RAW_RING)][:, :, :],
                                   high[kind][r][:, :, :].bitcast(F32), ALU.subtract).then_inc(s_low[kind], 1)

            def split_tail(s):
                pool.wait_ge(s_tail_high, number(s) + 2)
                pool.wait_ge(s_tail_used, number(s) + 1)
                pool.tensor_tensor(tail_parts[:, :], tail[:, :], tail_high[:, :].bitcast(F32),
                                   ALU.subtract).then_inc(s_tail_low, 1)

            def slot(s):
                quarter = (s[1] + 2) % TILES_PER_BLOCK
                b = s[0] + (s[1] + 2) // TILES_PER_BLOCK + 1
                left = list(range(FIELDS // TILES_PER_BLOCK)) if not isinstance(b, int) or b < BLOCKS else []
                items = plan.items(s)
                mine = of_kind(items, BY_POOL)
                if TAIL in items and not mine:
                    split_tail(s)
                for n, item in enumerate(mine):
                    split_low(s, item)
                    if TAIL in items and item == (2, 2):
                        split_tail(s)
                    if n == 1 and left and quarter == 0:
                        begin(b)
                    if n >= 1:
                        for _ in range(LOOKUPS_AFTER[n]):
                            if left:
                                look_up(FIELDS // TILES_PER_BLOCK * quarter + left.pop(0))
                for f in left:
                    look_up(FIELDS // TILES_PER_BLOCK * quarter + f)

            next_ids(0)
            for f in range(FIELDS):
                look_up(f)
            begin(1)
            for f in range(FIELDS // TILES_PER_BLOCK):
                look_up(f)
            for k in range(-1, START):
                slot((0, k))
            with pool.Fori(0, BLOCKS - 2) as i:
                for k in range(START, START + TILES_PER_BLOCK):
                    slot((i, k))
            for k in range(START, 2 * TILES_PER_BLOCK + 1):
                slot((BLOCKS - 2, k))

        @block.tensor
        def _(pe):
            def turn(n, chunks, rows, source):
                if n >= 2:
                    pe.wait_ge(s_stored, n - 1)
                for c in range(chunks):
                    last = pe.transpose(prep[n % 2][0:rows, c, :], source(c), ident[:, :])
                last.then_inc(s_turned, 1)

            pe.wait_ge(s_ident, 1)
            pe.wait_ge(s_sym, 7)
            turn(0, GROUP, P, lambda c: w0_dist[:, P * c:P * (c + 1)])
            turn(1, 1, P, lambda c: w0_dist[:, P * GROUP:P * (GROUP + 1)])
            pe.wait_ge(s_w1, 32)
            for g in range(GROUPS):
                turn(2 + g, GROUP, P, lambda c: w1_raw[:, P * (GROUP * g + c):P * (GROUP * g + c + 1)])
            pe.wait_ge(s_w2, 16)
            for g in range(GROUPS):
                turn(2 + GROUPS + g, GROUP, P, lambda c: w2_raw[:, P * (GROUP * g + c):P * (GROUP * g + c + 1)])
            pe.wait_ge(s_stored, PREP_GROUPS)

            def turn_x(t):
                pe.wait_ge(s_four, number(t) + 1)
                if not (isinstance(t[0], int) and number(t) == 0):
                    pe.wait_ge(s_xrows, number(t))
                    pe.wait_ge(s_made[kind_of(LAST0)], plan.entry(after(t, -2), LAST0) + 1)
                for e in range(QUAD):
                    last = pe.transpose(xT[:, P * e:P * (e + 1)],
                                        four_times[:, e, :, :].rearrange("p a f -> p (a f)"), ident[:, :])
                last.then_inc(s_xT, 1)

            def accumulator(s, layer):
                return y2[(s[1] - 1) % 2] if layer == 2 else (y0, y1)[layer]

            def begin_layer(s, layer):
                if layer == 0:
                    pe.wait_ge(s_h0, number(s) + 1)
                    pe.wait_ge(s_sum0, number(s) + 1)
                elif layer == 1:
                    pe.wait_ge(s_h1, number(s))
                    pe.wait_ge(s_sum1, number(s))
                elif not isinstance(s[0], int) or number(s) >= 2:
                    pe.wait_ge(s_sum2, number(s) - 2 + 1)

            def multiply(s, item):
                layer, n = item
                y = accumulator(s, layer)
                if n == 0:
                    begin_layer(s, layer)
                e, kind = plan.entry(s, item), kind_of(item)
                if kind == WHOLE:
                    z = prod[plan.place(s, item, RING)]
                    pe.wait_ge(s_made[kind], e + 1)
                    for c in range(ITEM):
                        last = pe.matmul(y[:, :], w1T[:, ITEM * n + c, :], z[:, c, :], start=(n == 0 and c == 0),
                                         stop=(item == LAST1 and c == ITEM - 1))
                    last.then_inc(s_used[kind], 1)
                else:
                    z = high[kind][plan.place(s, item, RING)]
                    pe.wait_ge(s_high[kind], e + 1)
                    for c in range(ITEM):
                        for w in ((w0T_high, w0T_low) if layer == 0 else (w2T_high, w2T_low)):
                            pe.matmul(y[:, :], w[:, ITEM * n + c, :], z[:, c, :],
                                      start=(n == 0 and c == 0 and w in (w0T_high, w2T_high)), stop=False)

            def multiply_low(s, item):
                layer, n = item
                if item == TAIL:
                    pe.wait_ge(s_tail_low, number(s) + 2)
                    pe.matmul(y0[:, :], w0T_tail[:, :], tail_parts[:, :], start=False, stop=False).then_inc(s_tail_used, 1)
                    return
                kind = kind_of(item)
                z = low[kind][plan.place(s, item, RING)]
                pe.wait_ge(s_low[kind], plan.entry(s, item) + 1)
                for c in range(ITEM):
                    last = pe.matmul(accumulator(s, layer)[:, :], (w0T_high if layer == 0 else w2T_high)[:, ITEM * n + c, :],
                                     z[:, c, :], start=False, stop=(item in (LAST0, LAST2) and c == ITEM - 1))
                last.then_inc(s_used[kind], 1)

            def slot(s, between={}):
                items = plan.items(s)
                nxt = after(s, 2)
                turn_after = (2, 4) if (2, 4) in items else items[-1]
                waiting = None
                for item in items:
                    if item != TAIL:
                        multiply(s, item)
                    if waiting:
                        multiply_low(s, waiting)
                    waiting = item if item == TAIL or kind_of(item) != WHOLE else None
                    if item in between:
                        between[item]()
                    if item == turn_after and (not isinstance(s[0], int) or number(nxt) < TILES):
                        if waiting and item == items[-1]:
                            multiply_low(s, waiting)
                            waiting = None
                        turn_x(nxt)
                if waiting:
                    multiply_low(s, waiting)

            turn_x((0, 0))
            for k in range(-1, START):
                slot((0, k))
            with pe.Fori(0, BLOCKS - 1) as i:
                for k in range(START, START + TILES_PER_BLOCK):
                    slot((i, k))
            for k in range(START, TILES_PER_BLOCK + 1):
                slot((BLOCKS - 1, k))

            banks = [y0, y1, h0[0], h1, xT, h0[1]]
            pe.wait_ge(s_dense, 16)
            pe.wait_ge(s_h1, TILES)
            for b in range(BLOCKS):
                last = pe.transpose((y0, xT)[b // GROUP][0:DENSE, P * (b % GROUP):P * (b % GROUP + 1)],
                                    dense_raw[:, DENSE * b:DENSE * (b + 1)], ident[:, :])
            last.then_inc(s_denseT, 1)
            pe.wait_ge(s_denseT, 2)
            pe.wait_ge(s_z, 2 * BLOCKS + 1)
            pe.wait_ge(s_top_w, 3 * 16)
            pe.wait_ge(s_top_b, 3 * 16)
            step = 0
            for n in range(2):
                rows = slice(TOP1 * n, TOP1 * (n + 1))
                for m in range(TOP1 // P):
                    if step >= len(banks):
                        pe.wait_ge(s_relu, step - len(banks) + 1)
                    bank = banks[step % len(banks)]
                    cols = slice(P * m, P * (m + 1))
                    pe.matmul(bank[:, :], wt1[:, 0, cols], z_kept[:, rows], start=True, stop=False)
                    pe.matmul(bank[:, :], wt1[:, 1, cols], z_last[:, rows], start=False, stop=False)
                    pe.matmul(bank[:, :], wt1_dense[:, cols], denseT[:, rows],
                              start=False, stop=True).then_inc(s_top, 1)
                    step += 1
            for n in range(2):
                pe.wait_ge(s_relu, TOP1 // P * (n + 1))
                for m in range(TOP2 // P):
                    pe.wait_ge(s_relu, step - len(banks) + 1)
                    bank = banks[step % len(banks)]
                    for c in range(TOP1 // P):
                        last = pe.matmul(bank[:, :], wt2[:, c, P * m:P * (m + 1)],
                                         hidden1[:, TOP1 // P * n + c, :], start=(c == 0), stop=(c == TOP1 // P - 1))
                    last.then_inc(s_top, 1)
                    step += 1
            for n in range(2):
                pe.wait_ge(s_relu, 2 * TOP1 // P + TOP2 // P * (n + 1))
                for c in range(TOP2 // P):
                    last = pe.matmul(y2[n][0:1, :], wt3[:, c:c + 1],
                                     hidden2[:, TOP2 // P * n + c, :], start=(c == 0), stop=(c == TOP2 // P - 1))
                last.then_inc(s_top, 1)

        @block.scalar
        def _(act):
            act.wait_ge(s_biases, 5 * 16)
            act.wait_ge(s_zero, 1)

            def take_rows(t):
                b = t[0] + t[1] // TILES_PER_BLOCK
                act.wait_ge(s_looked, 16 * FIELDS * (b + 1))
                act.copy(emb[:, :, :], looked_up[:, :, :]).then_inc(s_emb, 1)

            def repeat_fields(t):
                q = t[1] % TILES_PER_BLOCK
                act.wait_ge(s_emb, t[0] + t[1] // TILES_PER_BLOCK + 1)
                act.wait_ge(s_xT, number(t))
                act.copy(four_times[:, :, :, :],
                         emb[:, :, QUAD * q:QUAD * (q + 1)].rearrange("p f e -> p e f").unsqueeze(2).to_broadcast(
                             [P, QUAD, GROUP, FIELDS])).then_inc(s_four, 1)

            def take_x(t):
                act.wait_ge(s_xT, number(t) + 1)
                act.wait_ge(s_xcols, 16 * number(t))
                act.copy(xrows[:, :], xT[0:XROWS, :]).then_inc(s_xrows, 1)

            def go_on(h, y, half, bias, s_h):
                lanes = slice(half * HALF, half * HALF + HALF)
                for to in (slice(0, HALF), slice(HALF, P)):
                    last = act.activation(h[to, :], y[lanes, :], ACT.Relu, bias=bias[lanes, :])
                last.then_inc(s_h, 1)

            def split_high(s, item):
                e, kind = plan.entry(s, item), kind_of(item)
                act.wait_ge(s_made[kind], e + 1)
                if not isinstance(e, int) or e >= RING[kind]:
                    act.wait_ge(s_used[kind], e - RING[kind] + 1)
                act.copy(high[kind][plan.place(s, item, RING)][:, :, :],
                         unsplit[kind][plan.place(s, item, RAW_RING)][:, :, :]).then_inc(s_high[kind], 1)

            def next_h0(s):
                act.wait_ge(s_used[kind_of(LAST0)], plan.entry(s, LAST0) + 1)
                go_on(h0[(s[1] + 1) % 2], y0, 1, bias0, s_h0)

            def slot(s):
                items = plan.items(s)
                nxt = after(s, 2)
                more = not isinstance(s[0], int) or number(nxt) < TILES
                ready_after = (2, 0) if (2, 0) in items else None
                h0_after = (2, 4) if (2, 4) in items else None
                x_after = (2, 5) if (2, 5) in items else None
                if more and not ready_after:
                    if nxt[1] % TILES_PER_BLOCK == 0:
                        take_rows(nxt)
                    repeat_fields(nxt)
                for item in items:
                    if item == TAIL:
                        act.wait_ge(s_tail, number(s) + 2)
                        act.wait_ge(s_tail_low, number(s) + 1)
                        act.copy(tail[0:HALF, :].bitcast(F32R), tail[0:HALF, :])
                        act.copy(tail_high[HALF:P, :], tail[HALF:P, :]).then_inc(s_tail_high, 1)
                    elif kind_of(item) != WHOLE:
                        split_high(s, item)
                    if more and item == x_after:
                        take_x(nxt)
                    if item == h0_after and LAST0 in items:
                        next_h0(s)
                    if more and item == ready_after:
                        if nxt[1] % TILES_PER_BLOCK == 0:
                            take_rows(nxt)
                        repeat_fields(nxt)
                if h0_after is None and LAST0 in items:
                    next_h0(s)
                if more and x_after is None:
                    take_x(nxt)
                if LAST1 in items:
                    act.wait_ge(s_used[WHOLE], plan.entry(s, LAST1) + 1)
                    if LAST2 in items:
                        act.wait_ge(s_made[kind_of(LAST2)], plan.entry(s, LAST2) + 1)
                    go_on(h1, y1, 0, bias1, s_h1)

            take_rows((0, 0))
            repeat_fields((0, 0))
            take_x((0, 0))
            for k in range(-1, START):
                slot((0, k))
            with act.Fori(0, BLOCKS - 1) as i:
                for k in range(START, START + TILES_PER_BLOCK):
                    slot((i, k))
            for k in range(START, TILES_PER_BLOCK + 1):
                slot((BLOCKS - 1, k))

            banks = [y0, y1, h0[0], h1, xT, h0[1]]
            act.wait_ge(s_top_b, 3 * 16)
            act.wait_ge(s_denseT, 1)
            act.copy(denseT[:, 0:TOP1], y0[0:DENSE, :])
            act.copy(denseT[:, TOP1:2 * TOP1], xT[0:DENSE, :]).then_inc(s_denseT, 1)
            step = 0
            for n in range(2):
                for m in range(TOP1 // P):
                    act.wait_ge(s_top, step + 1)
                    act.activation(hidden1[:, TOP1 // P * n + m, :], banks[step % len(banks)][:, :], ACT.Relu,
                                   bias=bt1[:, m:m + 1]).then_inc(s_relu, 1)
                    step += 1
            for n in range(2):
                for m in range(TOP2 // P):
                    act.wait_ge(s_top, step + 1)
                    act.activation(hidden2[:, TOP2 // P * n + m, :], banks[step % len(banks)][:, :], ACT.Relu,
                                   bias=bt2[:, m:m + 1]).then_inc(s_relu, 1)
                    step += 1
            for n in range(2):
                act.wait_ge(s_top, step + 1)
                act.copy(y_rows[n][0:1, :],
                         y2[n][0:1, :]).then_inc(s_row, 1)
                step += 1

        @block.vector
        def _(dve):
            wide = w0_wide.rearrange("p (f g) -> p f g", g=2 * FIELDS)
            raw = w0_raw.rearrange("p (f g) -> p f g", g=FIELDS)
            dve.wait_ge(s_w0, 16)
            for n in range(2):
                dve.tensor_tensor(wide[:, :, FIELDS * n:FIELDS * (n + 1)], raw, raw.rearrange("p f g -> p g f"),
                                  ALU.add).then_inc(s_sym, 1)
            dve.wait_ge(s_sym, 2)

            def diagonal(ap, width, start, count):
                return bass.AP(ap.tensor, ap.offset + start, [list(ap.ap[0]), [width + 1, count]])

            H = FIELDS // 2
            dve.tensor_copy(w0_dist[:, FIELDS:FIELDS * H].rearrange("p (d f) -> p d f", f=FIELDS),
                            bass.AP(w0_wide.tensor, w0_wide.offset + 1,
                                    [list(w0_wide.ap[0]), [1, H - 1], [2 * FIELDS + 1, FIELDS]])).then_inc(s_sym, 1)
            dve.tensor_copy(w0_dist[:, 0:FIELDS], diagonal(w0_raw, FIELDS, 0, FIELDS)).then_inc(s_sym, 1)
            dve.tensor_copy(w0_dist[:, FIELDS * H:FIELDS * H + H],
                            diagonal(w0_raw, FIELDS, H, H)).then_inc(s_sym, 1)
            dve.tensor_copy(w0_dist[:, FIELDS * H + H:FIELDS * (H + 1)],
                            diagonal(w0_raw, FIELDS, H * FIELDS, H)).then_inc(s_sym, 1)
            dve.wait_ge(s_sym, 6)
            once = w0_dist[:, FIELDS * H:FIELDS * (H + 1)]
            dve.tensor_copy(w0_dist[:, FIELDS * (H + 1):FIELDS * (H + GROUP)].rearrange("p (a f) -> p a f", f=FIELDS),
                            once.unsqueeze(1).to_broadcast([P, GROUP - 1, FIELDS])).then_inc(s_sym, 1)
            homes = [w0T_high[:, :, :], w0T_tail[:, :]]
            homes += [w1T[:, GROUP * g:GROUP * (g + 1), :] for g in range(GROUPS)]
            homes += [w2T_high[:, GROUP * g:GROUP * (g + 1), :] for g in range(GROUPS)]
            lows = {0: w0T_low[:, :, :]}
            lows.update({2 + GROUPS + g: w2T_low[:, GROUP * g:GROUP * (g + 1), :] for g in range(GROUPS)})
            for n, home in enumerate(homes):
                dve.wait_ge(s_turned, n + 1)
                source = prep[1][:, 0, :] if n == 1 else prep[n % 2]
                if n == 1:
                    dve.tensor_copy(home, source).then_inc(s_tail_w, 1)
                    dve.wait_ge(s_tail_w, 1)
                    for quarter in (1, 3):
                        lanes = slice(FIELDS * quarter, FIELDS * (quarter + 1))
                        last = dve.tensor_tensor(w0T_tail[lanes, :], source[lanes, :],
                                                 w0T_tail[lanes, :].bitcast(F32), ALU.subtract)
                    last.then_inc(s_stored, 1)
                elif n in lows:
                    dve.tensor_copy(home, source).then_inc(s_w_high, 1)
                    dve.wait_ge(s_w_high, sorted(lows).index(n) + 1)
                    dve.tensor_tensor(lows[n], source, home.bitcast(F32), ALU.subtract).then_inc(s_stored, 1)
                else:
                    dve.tensor_copy(home, source).then_inc(s_stored, 1)
            dve.wait_ge(s_biases, 5 * 16)
            dve.tensor_scalar(neg_bias[:, :], bias_all[:, :], -1.0, None, ALU.mult).then_inc(s_neg, 1)
            dve.tensor_scalar(bias_sum[:, :], bias_all[:, :], float(EMBED), None, ALU.mult).then_inc(s_neg, 1)
            dve.wait_ge(s_neg, 2)
            dve.wait_ge(s_stored, PREP_GROUPS)
            dve.sem_inc(s_sum2, 1)
            dve.sem_inc(s_z, 1)

            def multiply(s, item):
                layer, n = item
                t = after(s, {0: 1, 1: 0, 2: -1}[layer])
                if item == (0, 0):
                    dve.wait_ge(s_shifted, 16 * GROUP * (number(t) + 1))
                    dve.wait_ge(s_xT, number(t) + 1)
                if item == TAIL:
                    dve.wait_ge(s_shifted_tail, 16 * GROUP * (number(t) + 1))
                    dve.wait_ge(s_tail_low, number(t))
                    dve.tensor_tensor(tail[:, :], shifted_tail[:, :], xT[:, :], ALU.mult).then_inc(s_tail, 1)
                    return
                x = shifted if layer == 0 else spread[t[1] % 2]
                b = (xT, h0[t[1] % 2], h1)[layer]
                if layer == 1:
                    if n == 0:
                        dve.wait_ge(s_h0, number(t) + 1)
                    if n % (GROUP // ITEM) == 0:
                        dve.wait_ge(s_spread[t[1] % 2][n // (GROUP // ITEM)], 32 * uses_of_parity(t))
                if item == (2, 0):
                    dve.wait_ge(s_h1, number(t) + 1)
                e, kind = plan.entry(s, item), kind_of(item)
                if kind == WHOLE:
                    if not isinstance(e, int) or e >= RING[kind]:
                        dve.wait_ge(s_used[kind], e - RING[kind] + 1)
                    z = prod[plan.place(s, item, RING)]
                else:
                    if not isinstance(e, int) or e >= RAW_RING[kind]:
                        dve.wait_ge(s_low[kind], e - RAW_RING[kind] + 1)
                    z = unsplit[kind][plan.place(s, item, RAW_RING)]
                dve.tensor_tensor(z[:, :, :], x[:, ITEM * n:ITEM * (n + 1), :],
                                  b[:, :].unsqueeze(1).to_broadcast([P, ITEM, COLS]), ALU.mult).then_inc(s_made[kind], 1)

            def split_low(s, item):
                e, kind = plan.entry(s, item), BY_DVE
                dve.wait_ge(s_high[kind], e + 1)
                r = plan.place(s, item, RING)
                dve.tensor_tensor(low[kind][r][:, :, :], unsplit[kind][plan.place(s, item, RAW_RING)][:, :, :],
                                  high[kind][r][:, :, :].bitcast(F32), ALU.subtract).then_inc(s_low[kind], 1)

            def add_up(acc, y, lanes, col, t, s_sum):
                first = 1 if s_sum is s_sum2 else 0
                if t[1] % TILES_PER_BLOCK == 0:
                    b = t[0] + t[1] // TILES_PER_BLOCK
                    if not isinstance(b, int) or b > 0:
                        dve.wait_ge(s_z, 2 * b + col)
                    dve.tensor_scalar(acc[lanes, :], y[lanes, :], neg_bias[lanes, col:col + 1], None,
                                      ALU.max).then_inc(s_sum, 1)
                else:
                    dve.wait_ge(s_sum, number(t) + first)
                    dve.scalar_tensor_tensor(out=acc[lanes, :], in0=y[lanes, :],
                                             scalar=neg_bias[lanes, col:col + 1], in1=acc[lanes, :],
                                             op0=ALU.max, op1=ALU.add).then_inc(s_sum, 1)

            def fold(acc, z, col, t, s_sum):
                b = t[0] + t[1] // TILES_PER_BLOCK
                first = 1 if s_sum is s_sum2 else 0
                dve.wait_ge(s_sum, number(t) + 1 + first)
                dve.tensor_tensor(acc[:, 0:COLS // 2], acc[:, 0:COLS // 2], acc[:, COLS // 2:COLS],
                                  ALU.add).then_inc(s_fold, 1)
                dve.wait_ge(s_fold, 2 * b + col + 1)
                dve.scalar_tensor_tensor(out=z[:, bass.ds(P * b, P)], in0=acc[:, 0:P],
                                         scalar=bias_sum[:, col:col + 1], in1=acc[:, P:2 * P],
                                         op0=ALU.add, op1=ALU.add).then_inc(s_z, 1)

            KEPT0, KEPT1, ALL = slice(0, HALF), slice(HALF, P), slice(0, P)

            def sum0(t):
                dve.wait_ge(s_used[kind_of(LAST0)], plan.entry(after(t, -1), LAST0) + 1)
                add_up(acc_kept, y0, KEPT0, 0, t, s_sum0)

            def sum1(t):
                dve.wait_ge(s_used[WHOLE], plan.entry(t, LAST1) + 1)
                add_up(acc_kept, y1, KEPT1, 0, t, s_sum1)

            def fold_kept(t):
                if t[1] % TILES_PER_BLOCK == TILES_PER_BLOCK - 1:
                    dve.wait_ge(s_sum0, number(t) + 1)
                    fold(acc_kept, z_kept, 0, t, s_sum1)

            def sum2(t):
                dve.wait_ge(s_used[kind_of(LAST2)], plan.entry(after(t, 1), LAST2) + 1)
                add_up(acc_last, y2[t[1] % 2], ALL, 1, t, s_sum2)
                if t[1] % TILES_PER_BLOCK == TILES_PER_BLOCK - 1:
                    fold(acc_last, z_last, 1, t, s_sum2)

            def slot(s):
                waiting = None
                for item in plan.items(s):
                    mine = item != TAIL and kind_of(item) == BY_DVE
                    if waiting and mine:
                        split_low(s, waiting)
                        waiting = None
                    if item == (2, 0):
                        sum1(after(s, -1))
                    multiply(s, item)
                    if waiting:
                        split_low(s, waiting)
                    waiting = item if mine else None
                    if item == (2, 0):
                        fold_kept(after(s, -1))
                    if item == (1, 2):
                        sum0(s)
                    if item == (2, 3) and s[1] >= START:
                        sum2(after(s, -2))
                if waiting:
                    split_low(s, waiting)

            for k in range(-1, START):
                slot((0, k))
            with dve.Fori(0, BLOCKS - 1) as i:
                for k in range(START, START + TILES_PER_BLOCK):
                    slot((i, k))
            for k in range(START, TILES_PER_BLOCK + 1):
                slot((BLOCKS - 1, k))
            sum2((BLOCKS - 1, TILES_PER_BLOCK - 1))


TABLES = FIELDS


def kernel(**inputs):
    import numpy as np
    import concourse.bacc as bacc
    from concourse.bass_utils import run_bass_kernel_spmd

    nc = bacc.Bacc("TRN2", target_bir_lowering=False, num_devices=1)
    arrays = {}

    def dram(name):
        a = np.ascontiguousarray(inputs[name])
        arrays["in_" + name] = a
        return nc.dram_tensor("in_" + name, a.shape, mybir.dt.from_np(a.dtype), kind="ExternalInput").ap()

    batch = inputs["ids"].shape[0]
    tiles = batch // P * TILES_PER_BLOCK
    tables = [dram(f"tbl_{f}") for f in range(TABLES)]
    xcols = nc.dram_tensor("xcols", (tiles, XROWS, COLS), F32, kind="Internal").ap()
    out = nc.dram_tensor("out", (batch, 1), F32, kind="ExternalOutput").ap()
    dlrm_tower(nc, dram("dense_ctx"), dram("ids"), tables, dram("W_top1"), dram("b_top1"),
               dram("W_top2"), dram("b_top2"), dram("W_top3"), dram("L0_rec_W0"), dram("L0_rec_b0"),
               dram("L0_rec_W1"), dram("L0_rec_b1"), dram("L0_rec_W2"), dram("L0_rec_b2"), xcols, out)
    result = run_bass_kernel_spmd(nc, [arrays], core_ids=[0])
    return result.results[0]["out"]
```

```python
from contextlib import ExitStack

import concourse.bass as bass
from concourse import mybir

ALU = mybir.AluOpType
AXIS = mybir.AxisListType
ACT = mybir.ActivationFunctionType
F32 = mybir.dt.float32
F32R = mybir.dt.float32r
I32 = mybir.dt.int32
U32 = mybir.dt.uint32

P = 128
FIELDS = 32
EMBED = 16
HALF = 64
QUAD = 4
COLS = QUAD * P
TILES_PER_BLOCK = EMBED // QUAD
ITEM = 2
GROUP = 4
CHUNKS = FIELDS * HALF // P
GROUPS = CHUNKS // GROUP
ITEMS = CHUNKS // ITEM
XROWS = FIELDS + FIELDS // 2
DENSE = 16
TOP1, TOP2 = 512, 256


def number(t):
    return TILES_PER_BLOCK * t[0] + t[1]


def after(t, n):
    return (t[0], t[1] + n)


def uses_of_parity(t):
    return TILES_PER_BLOCK // 2 * t[0] + t[1] // 2 + 1


TAIL = (0, -1)
SLOT = [(1, 0), (1, 1), (2, 0), (1, 2), (2, 1), (1, 3), (0, 0), (2, 2), TAIL, (1, 4), (0, 1),
        (2, 3), (1, 5), (2, 4), (1, 6), (2, 5), (1, 7), (2, 6), (2, 7)]
START = 2

WHOLE, BY_POOL, BY_DVE = range(3)
SPLIT = (BY_POOL, BY_DVE)
RING = (4, 4, 2)


ADD_KEPT_AFTER = (2, 1)
FOLD_KEPT_AFTER = (2, 2)
LOOKUPS_AFTER = (0, 1, 2, 1, 1, 2, 1)


def kind_of(item):
    if item[0] == 1:
        return WHOLE
    return BY_DVE if item[0] == 0 or item == (2, 6) else BY_POOL


def slot_items(n, tiles):
    tile = {0: n + 1, 1: n, 2: n - 1}
    return [x for x in SLOT if 0 <= tile[x[0]] < tiles]


def of_kind(items, kind):
    return [x for x in items if x != TAIL and kind_of(x) == kind]


class Plan:

    def __init__(self, tiles):
        self.tiles = tiles
        self.steady = [len(of_kind(SLOT, kind)) for kind in (WHOLE, *SPLIT)]
        assert all(TILES_PER_BLOCK * n % ring == 0 for n, ring in zip(self.steady, RING))

    def items(self, s):
        return slot_items(number(s), self.tiles) if isinstance(s[0], int) else SLOT

    def before(self, kind, n):
        return sum(len(of_kind(slot_items(m, self.tiles), kind)) for m in range(-1, n))

    def entry(self, s, item):
        kind = kind_of(item)
        rank = of_kind(self.items(s), kind).index(item)
        if isinstance(s[0], int):
            return self.before(kind, number(s)) + rank
        return TILES_PER_BLOCK * self.steady[kind] * s[0] + self.before(kind, s[1]) + rank

    def place(self, s, item, ring):
        kind = kind_of(item)
        if isinstance(s[0], int):
            return self.entry(s, item) % ring[kind]
        return (self.before(kind, s[1]) + of_kind(SLOT, kind).index(item)) % ring[kind]


def dlrm_tower(nc, dense_ctx, ids, tables, w_top1, b_top1, w_top2, b_top2, w_top3,
               w0, b0, w1, b1, w2, b2, xcols, out):
    batch = ids.shape[0]
    BLOCKS = batch // P
    TILES = BLOCKS * TILES_PER_BLOCK
    assert len(tables) == FIELDS
    plan = Plan(TILES)
    LAST0, LAST1, LAST2 = (0, GROUP // ITEM - 1), (1, ITEMS - 1), (2, ITEMS - 1)

    with ExitStack() as ctx:
        def sb(name, shape, dt=F32):
            return ctx.enter_context(nc.sbuf_tensor(name, shape, dt))

        def ps(name, shape):
            return ctx.enter_context(nc.psum_tensor(name, shape, F32))

        def sem(name):
            return ctx.enter_context(nc.semaphore(name))

        w0T_high = sb("w0T_high", [P, GROUP, P], F32R)
        w0T_low = sb("w0T_low", [P, GROUP, P], F32R)
        w0T_tail = sb("w0T_tail", [P, P], F32R)
        w1T = sb("w1T", [P, CHUNKS, P])
        w2T_high = sb("w2T_high", [P, CHUNKS, P], F32R)
        w2T_low = sb("w2T_low", [P, CHUNKS, P], F32R)
        wt3 = sb("wt3", [P, TOP2 // P])
        ident = sb("ident", [P, P])
        bias0 = sb("bias0", [P, 1])
        bias1 = sb("bias1", [P, 1])
        bias_kept = sb("bias_kept", [P, 1])
        bias_last = sb("bias_last", [P, 1])
        neg_last = sb("neg_last", [P, 1])
        last_tiles = sb("last_tiles", [P, 1])
        bt1 = sb("bt1", [P, TOP1 // P])
        bt2 = sb("bt2", [P, TOP2 // P])
        ids_sb = sb("ids_sb", [P, BLOCKS, FIELDS], I32)
        ids_now = sb("ids_now", [P, FIELDS], I32)
        looked_up = sb("looked_up", [P, FIELDS, EMBED])
        emb = sb("emb", [P, FIELDS, EMBED])
        four_times = sb("four_times", [P, QUAD, GROUP, FIELDS])
        xrows = sb("xrows", [XROWS, COLS])
        shifted = sb("shifted", [P, GROUP, COLS])
        shifted_tail = sb("shifted_tail", [P, COLS])
        spread = [sb(f"spread{p}", [P, CHUNKS, COLS]) for p in range(2)]
        prod = [sb(f"prod{r}", [P, ITEM, COLS]) for r in range(RING[WHOLE])]
        tail = sb("tail", [P, COLS])
        tail_high = sb("tail_high", [P, COLS], F32R)
        tail_parts = sb("tail_parts", [P, COLS], F32R)
        high = [None] + [[sb(f"high{kind}{r}", [P, ITEM, COLS], F32R) for r in range(RING[kind])]
                         for kind in SPLIT]
        unsplit, low = [None], [None]
        for kind in SPLIT:
            unsplit.append([])
            low.append([])
            for r in range(RING[kind]):
                unsplit[kind].append(sb(f"unsplit{kind}{r}", [P, ITEM, COLS]))
                low[kind].append(nc.alloc_sbuf_tensor_at(f"low{kind}{r}", [P, ITEM, COLS], F32R,
                                                         offset=nc.sbuf_base - ITEM * COLS * mybir.dt.size(F32)))
        kept = [sb(f"kept{p}", [P, COLS]) for p in range(2)]
        acc_kept = sb("acc_kept", [P, COLS])
        acc_last = sb("acc_last", [P, COLS])
        z_kept = sb("z_kept", [P, batch])
        z_last = sb("z_last", [P, batch])

        y0 = ps("y0", [P, COLS])
        y1 = ps("y1", [P, COLS])
        y2 = [ps(f"y2_{p}", [P, COLS]) for p in range(2)]
        h0 = [ps(f"h0_{p}", [P, COLS]) for p in range(2)]
        h1 = ps("h1", [P, COLS])
        xT = ps("xT", [P, COLS])
        prep = [bank[:, :].rearrange("p (a b) -> p a b", b=P) for bank in y2]

        s_ids = sem("s_ids")
        s_w0 = sem("s_w0")
        s_w1 = sem("s_w1")
        s_w2 = sem("s_w2")
        s_dense = sem("s_dense")
        s_biases = sem("s_biases")
        s_top_w = sem("s_top_w")
        s_top_b = sem("s_top_b")
        s_ones = sem("s_ones")
        s_zero = sem("s_zero")
        s_ident = sem("s_ident")
        s_neg = sem("s_neg")
        s_sym = sem("s_sym")
        s_turned = sem("s_turned")
        s_stored = sem("s_stored")
        s_w_high = sem("s_w_high")
        s_tail_w = sem("s_tail_w")
        s_denseT = sem("s_denseT")
        s_now = sem("s_now")
        s_block = sem("s_block")
        s_looked = sem("s_looked")
        s_emb = sem("s_emb")
        s_four = sem("s_four")
        s_xT = sem("s_xT")
        s_xrows = sem("s_xrows")
        s_xcols = sem("s_xcols")
        s_shifted = sem("s_shifted")
        s_shifted_tail = sem("s_shifted_tail")
        s_spread = [[sem(f"s_spread{p}{g}") for g in range(GROUPS)] for p in range(2)]
        s_made = [sem(f"s_made{kind}") for kind in (WHOLE, *SPLIT)]
        s_high = [None] + [sem(f"s_high{kind}") for kind in SPLIT]
        s_low = [None] + [sem(f"s_low{kind}") for kind in SPLIT]
        s_used = [sem(f"s_used{kind}") for kind in (WHOLE, *SPLIT)]
        s_tail = sem("s_tail")
        s_tail_high = sem("s_tail_high")
        s_tail_low = sem("s_tail_low")
        s_tail_used = sem("s_tail_used")
        s_h0 = sem("s_h0")
        s_h1 = sem("s_h1")
        s_kept0 = sem("s_kept0")
        s_kept1 = sem("s_kept1")
        s_sum_kept = sem("s_sum_kept")
        s_sum2 = sem("s_sum2")
        s_z = sem("s_z")
        s_top = sem("s_top")
        s_relu = sem("s_relu")
        s_row = sem("s_row")
        s_out = sem("s_out")

        flat = lambda ap: ap.rearrange("p a b -> p (a b)")
        w1_raw = flat(spread[0][:, 0:4, :])
        w2_raw = flat(spread[0][:, 4:8, :])
        w0_raw = flat(spread[0][:, 8:10, :])
        w0_wide = flat(spread[0][:, 10:14, :])
        w0_dist = flat(spread[0][:, 14:16, :])
        hidden1 = spread[0][:, 0:8, :]
        wt1 = spread[0][:, 8:10, :]
        wt2 = flat(spread[0][:, 10:12, :]).rearrange("p (c n) -> p c n", n=TOP2)
        wt1_dense = spread[0][0:DENSE, 12, :]
        denseT = flat(spread[0][0:DENSE, 13:15, :])
        dense_raw = spread[0][:, 15, 0:BLOCKS * DENSE]
        hidden2 = spread[1]
        y_rows = [acc_kept, acc_last]

        PREP_GROUPS = 2 + 2 * GROUPS

        block = ctx.enter_context(nc.Block())

        @block.sync
        def _(sp):
            sp.dma_start(ids_sb[:, :, :], ids.rearrange("(n p) f -> p n f", p=P)).then_inc(s_ids, 16)
            sp.dma_start(w0_raw, w0[:, :]).then_inc(s_w0, 16)
            sp.dma_start(w1_raw[0:HALF, :], w1[HALF:P, :]).then_inc(s_w1, 16)
            sp.dma_start(w1_raw[HALF:P, :], w1[0:HALF, :]).then_inc(s_w1, 16)
            sp.dma_start(w2_raw, w2[:, :]).then_inc(s_w2, 16)
            for to, of in ((bias0[HALF:P, :], b0[HALF:P]), (bias1[0:HALF, :], b1[HALF:P]),
                           (bias_kept[0:HALF, :], b0[0:HALF]), (bias_kept[HALF:P, :], b1[0:HALF]),
                           (bias_last[:, :], b2)):
                sp.dma_start(to, of.rearrange("(p a) -> p a", a=1)).then_inc(s_biases, 16)

            def load_shifted(t):
                sp.wait_ge(s_xrows, number(t) + 1)
                sp.dma_start(xcols[number(t)], xrows[:, :]).then_inc(s_xcols, 16)
                sp.wait_ge(s_xcols, 16 * (number(t) + 1))
                x = xcols[number(t)]
                for j in range(GROUP):
                    sp.dma_start(shifted[FIELDS * j:FIELDS * (j + 1), :, :],
                                 bass.AP(x.tensor, x.offset + j * COLS,
                                         [[COLS, FIELDS], [GROUP * COLS, GROUP], [1, COLS]])
                                 ).then_inc(s_shifted, 16)
                for j in range(GROUP):
                    sp.dma_start(shifted_tail[FIELDS * j:FIELDS * (j + 1), :],
                                 x[FIELDS // 2:XROWS, :]).then_inc(s_shifted_tail, 16)

            def load_spread(t, g):
                x = xcols[number(t)]
                k = t[1]
                if not (isinstance(t[0], int) and number(t) < 2):
                    item = (2, GROUP // ITEM * (g + 1) - 1)
                    sp.wait_ge(s_made[kind_of(item)], plan.entry(after(t, -1), item) + 1)
                for half in range(2):
                    sp.dma_start(spread[k % 2][HALF * half:HALF * (half + 1), GROUP * g:GROUP * (g + 1), :],
                                 bass.AP(x.tensor, x.offset + (2 * GROUP * g + half) * COLS,
                                         [[0, HALF], [2 * COLS, GROUP], [1, COLS]])
                                 ).then_inc(s_spread[k % 2][g], 16)

            def load_factors(t):
                load_shifted(t)
                if not isinstance(t[0], int) or number(t) >= 1:
                    load_spread(after(t, -1), GROUPS - 1)
                for g in range(GROUPS - 1):
                    load_spread(t, g)

            sp.dma_start(wt3[:, :], w_top3.rearrange("(c p) n -> p (c n)", p=P), allow_slow_non_contiguous=True).then_inc(s_top_b, 16)
            sp.dma_start(bt1[:, :], b_top1.rearrange("(c p) -> p c", p=P), allow_slow_non_contiguous=True).then_inc(s_top_b, 16)
            sp.dma_start(bt2[:, :], b_top2.rearrange("(c p) -> p c", p=P), allow_slow_non_contiguous=True).then_inc(s_top_b, 16)
            sp.wait_ge(s_stored, PREP_GROUPS)
            load_factors((0, 0))
            load_factors((0, 1))
            load_factors((0, 2))
            with sp.Fori(0, BLOCKS - 1) as i:
                for k in range(START, START + TILES_PER_BLOCK):
                    load_factors((i, k + 1))
            load_factors((BLOCKS - 1, START + 1))
            load_spread((BLOCKS - 1, START + 1), GROUPS - 1)
            sp.wait_ge(s_made[kind_of(LAST2)], plan.entry((BLOCKS - 1, TILES_PER_BLOCK - 1), LAST2) + 1)
            sp.dma_start(dense_raw.rearrange("p (n c) -> p n c", c=DENSE),
                         dense_ctx.rearrange("(n p) c -> p n c", p=P)).then_inc(s_dense, 16)
            sp.dma_start(wt1, w_top1[0:2 * P, :].rearrange("(c p) n -> p c n", p=P)).then_inc(s_top_w, 16)
            sp.dma_start(wt1_dense, w_top1[2 * P:2 * P + DENSE, :]).then_inc(s_top_w, 16)
            sp.dma_start(wt2, w_top2.rearrange("(c p) n -> p c n", p=P)).then_inc(s_top_w, 16)
            for n in range(2):
                sp.wait_ge(s_row, n + 1)
                sp.dma_start(out.rearrange("b a -> a b")[:, TOP1 * n:TOP1 * (n + 1)],
                             y_rows[n][0:1, :]).then_inc(s_out, 16)
            sp.wait_ge(s_out, 32)

        @block.gpsimd
        def _(pool):
            pool.memset(ident[:, :], 0.0).then_inc(s_ones, 1)
            pool.wait_ge(s_ones, 1)
            pool.affine_select(out=ident[:, :], in_=ident[:, :], compare_op=ALU.not_equal, fill=1.0,
                               base=0, pattern=[[-1, P]], channel_multiplier=1).then_inc(s_ident, 1)
            pool.memset(tail_high[:, :].bitcast(F32), 0.0).then_inc(s_zero, 1)
            pool.wait_ge(s_ids, 16)

            def next_ids(b):
                pool.tensor_copy(ids_now[:, :], ids_sb[:, bass.ds(b, 1), :]).then_inc(s_now, 1)
                pool.wait_ge(s_now, b + 1)
                pool.sem_inc(s_block, 1)

            def begin(b):
                pool.wait_ge(s_looked, 16 * FIELDS * b)
                pool.wait_ge(s_emb, b)
                next_ids(b)

            def look_up(f):
                pool.indirect_dma_start(
                    out=looked_up[:, f, :], out_offset=None, in_=tables[f][:, :],
                    in_offset=bass.IndirectOffsetOnAxis(ap=ids_now[:, f:f + 1].bitcast(U32), axis=0),
                ).then_inc(s_looked, 16)

            def split_low(s, item):
                e, kind = plan.entry(s, item), BY_POOL
                pool.wait_ge(s_high[kind], e + 1)
                r = plan.place(s, item, RING)
                pool.tensor_tensor(low[kind][r][:, :, :], unsplit[kind][r][:, :, :],
                                   high[kind][r][:, :, :].bitcast(F32), ALU.subtract).then_inc(s_low[kind], 1)

            def split_tail(s):
                pool.wait_ge(s_tail_high, number(s) + 2)
                pool.wait_ge(s_tail_used, number(s) + 1)
                pool.tensor_tensor(tail_parts[:, :], tail[:, :], tail_high[:, :].bitcast(F32),
                                   ALU.subtract).then_inc(s_tail_low, 1)

            def slot(s):
                quarter = (s[1] + 2) % TILES_PER_BLOCK
                b = s[0] + (s[1] + 2) // TILES_PER_BLOCK + 1
                left = list(range(FIELDS // TILES_PER_BLOCK)) if not isinstance(b, int) or b < BLOCKS else []
                items = plan.items(s)
                mine = of_kind(items, BY_POOL)
                if TAIL in items and not mine:
                    split_tail(s)
                for n, item in enumerate(mine):
                    split_low(s, item)
                    if TAIL in items and item == (2, 2):
                        split_tail(s)
                    if n == 1 and left and quarter == 0:
                        begin(b)
                    if n >= 1:
                        for _ in range(LOOKUPS_AFTER[n]):
                            if left:
                                look_up(FIELDS // TILES_PER_BLOCK * quarter + left.pop(0))
                for f in left:
                    look_up(FIELDS // TILES_PER_BLOCK * quarter + f)

            next_ids(0)
            for f in range(FIELDS):
                look_up(f)
            begin(1)
            for f in range(FIELDS // TILES_PER_BLOCK):
                look_up(f)
            for k in range(-1, START):
                slot((0, k))
            with pool.Fori(0, BLOCKS - 2) as i:
                for k in range(START, START + TILES_PER_BLOCK):
                    slot((i, k))
            for k in range(START, 2 * TILES_PER_BLOCK + 1):
                slot((BLOCKS - 2, k))

        @block.tensor
        def _(pe):
            def turn(n, chunks, rows, source):
                if n >= 2:
                    pe.wait_ge(s_stored, n - 1)
                for c in range(chunks):
                    last = pe.transpose(prep[n % 2][0:rows, c, :], source(c), ident[:, :])
                last.then_inc(s_turned, 1)

            pe.wait_ge(s_ident, 1)
            pe.wait_ge(s_sym, 7)
            turn(0, GROUP, P, lambda c: w0_dist[:, P * c:P * (c + 1)])
            turn(1, 1, P, lambda c: w0_dist[:, P * GROUP:P * (GROUP + 1)])
            pe.wait_ge(s_w1, 32)
            for g in range(GROUPS):
                turn(2 + g, GROUP, P, lambda c: w1_raw[:, P * (GROUP * g + c):P * (GROUP * g + c + 1)])
            pe.wait_ge(s_w2, 16)
            for g in range(GROUPS):
                turn(2 + GROUPS + g, GROUP, P, lambda c: w2_raw[:, P * (GROUP * g + c):P * (GROUP * g + c + 1)])
            pe.wait_ge(s_stored, PREP_GROUPS)

            def turn_x(t):
                pe.wait_ge(s_four, number(t) + 1)
                if not (isinstance(t[0], int) and number(t) == 0):
                    pe.wait_ge(s_xrows, number(t))
                    pe.wait_ge(s_made[kind_of(LAST0)], plan.entry(after(t, -2), LAST0) + 1)
                for e in range(QUAD):
                    last = pe.transpose(xT[:, P * e:P * (e + 1)],
                                        four_times[:, e, :, :].rearrange("p a f -> p (a f)"), ident[:, :])
                last.then_inc(s_xT, 1)

            def accumulator(s, layer):
                return y2[(s[1] - 1) % 2] if layer == 2 else (y0, y1)[layer]

            def begin_layer(s, layer):
                if layer == 0:
                    pe.wait_ge(s_kept0, number(s) + 1)
                elif layer == 1:
                    pe.wait_ge(s_kept1, number(s))
                elif not isinstance(s[0], int) or number(s) >= 2:
                    pe.wait_ge(s_sum2, number(s) - 2 + 1)

            def multiply(s, item):
                layer, n = item
                y = accumulator(s, layer)
                if n == 0:
                    begin_layer(s, layer)
                e, kind = plan.entry(s, item), kind_of(item)
                if kind == WHOLE:
                    z = prod[plan.place(s, item, RING)]
                    pe.wait_ge(s_made[kind], e + 1)
                    for c in range(ITEM):
                        last = pe.matmul(y[:, :], w1T[:, ITEM * n + c, :], z[:, c, :], start=(n == 0 and c == 0),
                                         stop=(item == LAST1 and c == ITEM - 1))
                    last.then_inc(s_used[kind], 1)
                else:
                    z = high[kind][plan.place(s, item, RING)]
                    pe.wait_ge(s_high[kind], e + 1)
                    for c in range(ITEM):
                        for w in ((w0T_high, w0T_low) if layer == 0 else (w2T_high, w2T_low)):
                            pe.matmul(y[:, :], w[:, ITEM * n + c, :], z[:, c, :],
                                      start=(n == 0 and c == 0 and w in (w0T_high, w2T_high)), stop=False)

            def multiply_low(s, item):
                layer, n = item
                if item == TAIL:
                    pe.wait_ge(s_tail_low, number(s) + 2)
                    pe.matmul(y0[:, :], w0T_tail[:, :], tail_parts[:, :], start=False, stop=False).then_inc(s_tail_used, 1)
                    return
                kind = kind_of(item)
                z = low[kind][plan.place(s, item, RING)]
                pe.wait_ge(s_low[kind], plan.entry(s, item) + 1)
                for c in range(ITEM):
                    last = pe.matmul(accumulator(s, layer)[:, :], (w0T_high if layer == 0 else w2T_high)[:, ITEM * n + c, :],
                                     z[:, c, :], start=False, stop=(item in (LAST0, LAST2) and c == ITEM - 1))
                last.then_inc(s_used[kind], 1)

            def slot(s, between={}):
                items = plan.items(s)
                nxt = after(s, 2)
                turn_after = (2, 4) if (2, 4) in items else items[-1]
                waiting = None
                for item in items:
                    if item != TAIL:
                        multiply(s, item)
                    if waiting:
                        multiply_low(s, waiting)
                    waiting = item if item == TAIL or kind_of(item) != WHOLE else None
                    if item in between:
                        between[item]()
                    if item == turn_after and (not isinstance(s[0], int) or number(nxt) < TILES):
                        if waiting and item == items[-1]:
                            multiply_low(s, waiting)
                            waiting = None
                        turn_x(nxt)
                if waiting:
                    multiply_low(s, waiting)

            turn_x((0, 0))
            for k in range(-1, START):
                slot((0, k))
            with pe.Fori(0, BLOCKS - 1) as i:
                for k in range(START, START + TILES_PER_BLOCK):
                    slot((i, k))
            for k in range(START, TILES_PER_BLOCK + 1):
                slot((BLOCKS - 1, k))

            banks = [y0, y1, h0[0], h1, xT, h0[1]]
            pe.wait_ge(s_dense, 16)
            pe.wait_ge(s_kept1, TILES)
            for b in range(BLOCKS):
                last = pe.transpose((y0, xT)[b // GROUP][0:DENSE, P * (b % GROUP):P * (b % GROUP + 1)],
                                    dense_raw[:, DENSE * b:DENSE * (b + 1)], ident[:, :])
            last.then_inc(s_denseT, 1)
            pe.wait_ge(s_denseT, 2)
            pe.wait_ge(s_z, 2 * BLOCKS + 1)
            pe.wait_ge(s_top_w, 3 * 16)
            pe.wait_ge(s_top_b, 3 * 16)
            step = 0
            for n in range(2):
                rows = slice(TOP1 * n, TOP1 * (n + 1))
                for m in range(TOP1 // P):
                    if step >= len(banks):
                        pe.wait_ge(s_relu, step - len(banks) + 1)
                    bank = banks[step % len(banks)]
                    cols = slice(P * m, P * (m + 1))
                    pe.matmul(bank[:, :], wt1[:, 0, cols], z_kept[:, rows], start=True, stop=False)
                    pe.matmul(bank[:, :], wt1[:, 1, cols], z_last[:, rows], start=False, stop=False)
                    pe.matmul(bank[:, :], wt1_dense[:, cols], denseT[:, rows],
                              start=False, stop=True).then_inc(s_top, 1)
                    step += 1
            for n in range(2):
                pe.wait_ge(s_relu, TOP1 // P * (n + 1))
                for m in range(TOP2 // P):
                    pe.wait_ge(s_relu, step - len(banks) + 1)
                    bank = banks[step % len(banks)]
                    for c in range(TOP1 // P):
                        last = pe.matmul(bank[:, :], wt2[:, c, P * m:P * (m + 1)],
                                         hidden1[:, TOP1 // P * n + c, :], start=(c == 0), stop=(c == TOP1 // P - 1))
                    last.then_inc(s_top, 1)
                    step += 1
            for n in range(2):
                pe.wait_ge(s_relu, 2 * TOP1 // P + TOP2 // P * (n + 1))
                for c in range(TOP2 // P):
                    last = pe.matmul(y2[n][0:1, :], wt3[:, c:c + 1],
                                     hidden2[:, TOP2 // P * n + c, :], start=(c == 0), stop=(c == TOP2 // P - 1))
                last.then_inc(s_top, 1)

        @block.scalar
        def _(act):
            act.wait_ge(s_biases, 5 * 16)
            act.wait_ge(s_zero, 1)

            def take_rows(t):
                b = t[0] + t[1] // TILES_PER_BLOCK
                act.wait_ge(s_looked, 16 * FIELDS * (b + 1))
                act.copy(emb[:, :, :], looked_up[:, :, :]).then_inc(s_emb, 1)

            def repeat_fields(t):
                q = t[1] % TILES_PER_BLOCK
                act.wait_ge(s_emb, t[0] + t[1] // TILES_PER_BLOCK + 1)
                act.wait_ge(s_xT, number(t))
                act.copy(four_times[:, :, :, :],
                         emb[:, :, QUAD * q:QUAD * (q + 1)].rearrange("p f e -> p e f").unsqueeze(2).to_broadcast(
                             [P, QUAD, GROUP, FIELDS])).then_inc(s_four, 1)

            def take_x(t):
                act.wait_ge(s_xT, number(t) + 1)
                act.wait_ge(s_xcols, 16 * number(t))
                act.copy(xrows[:, :], xT[0:XROWS, :]).then_inc(s_xrows, 1)

            def go_on(h, y, half, bias, s_h):
                lanes = slice(half * HALF, half * HALF + HALF)
                for to in (slice(0, HALF), slice(HALF, P)):
                    last = act.activation(h[to, :], y[lanes, :], ACT.Relu, bias=bias[lanes, :])
                last.then_inc(s_h, 1)

            def keep(t, y, half, s_kept):
                lanes = slice(half * HALF, half * HALF + HALF)
                act.activation(kept[t[1] % 2][lanes, :], y[lanes, :], ACT.Relu,
                               bias=bias_kept[lanes, :]).then_inc(s_kept, 1)

            def split_high(s, item):
                e, kind = plan.entry(s, item), kind_of(item)
                act.wait_ge(s_made[kind], e + 1)
                r = plan.place(s, item, RING)
                act.copy(high[kind][r][:, :, :], unsplit[kind][r][:, :, :]).then_inc(s_high[kind], 1)

            def next_h0(s):
                act.wait_ge(s_used[kind_of(LAST0)], plan.entry(s, LAST0) + 1)
                go_on(h0[(s[1] + 1) % 2], y0, 1, bias0, s_h0)
                if not isinstance(s[0], int) or number(s) >= 1:
                    act.wait_ge(s_sum_kept, number(s))
                keep(after(s, 1), y0, 0, s_kept0)

            def slot(s):
                items = plan.items(s)
                nxt = after(s, 2)
                more = not isinstance(s[0], int) or number(nxt) < TILES
                ready_after = (2, 0) if (2, 0) in items else None
                h0_after = (2, 4) if (2, 4) in items else None
                x_after = (2, 5) if (2, 5) in items else None
                if more and not ready_after:
                    if nxt[1] % TILES_PER_BLOCK == 0:
                        take_rows(nxt)
                    repeat_fields(nxt)
                for item in items:
                    if item == TAIL:
                        act.wait_ge(s_tail, number(s) + 2)
                        act.wait_ge(s_tail_low, number(s) + 1)
                        act.copy(tail[0:HALF, :].bitcast(F32R), tail[0:HALF, :])
                        act.copy(tail_high[HALF:P, :], tail[HALF:P, :]).then_inc(s_tail_high, 1)
                    elif kind_of(item) != WHOLE:
                        split_high(s, item)
                    if more and item == x_after:
                        take_x(nxt)
                    if item == h0_after and LAST0 in items:
                        next_h0(s)
                    if more and item == ready_after:
                        if nxt[1] % TILES_PER_BLOCK == 0:
                            take_rows(nxt)
                        repeat_fields(nxt)
                if h0_after is None and LAST0 in items:
                    next_h0(s)
                if more and x_after is None:
                    take_x(nxt)
                if LAST1 in items:
                    act.wait_ge(s_used[WHOLE], plan.entry(s, LAST1) + 1)
                    if LAST2 in items:
                        act.wait_ge(s_made[kind_of(LAST2)], plan.entry(s, LAST2) + 1)
                    go_on(h1, y1, 0, bias1, s_h1)
                    keep(s, y1, 1, s_kept1)

            take_rows((0, 0))
            repeat_fields((0, 0))
            take_x((0, 0))
            for k in range(-1, START):
                slot((0, k))
            with act.Fori(0, BLOCKS - 1) as i:
                for k in range(START, START + TILES_PER_BLOCK):
                    slot((i, k))
            for k in range(START, TILES_PER_BLOCK + 1):
                slot((BLOCKS - 1, k))

            banks = [y0, y1, h0[0], h1, xT, h0[1]]
            act.wait_ge(s_top_b, 3 * 16)
            act.wait_ge(s_denseT, 1)
            act.copy(denseT[:, 0:TOP1], y0[0:DENSE, :])
            act.copy(denseT[:, TOP1:2 * TOP1], xT[0:DENSE, :]).then_inc(s_denseT, 1)
            step = 0
            for n in range(2):
                for m in range(TOP1 // P):
                    act.wait_ge(s_top, step + 1)
                    act.activation(hidden1[:, TOP1 // P * n + m, :], banks[step % len(banks)][:, :], ACT.Relu,
                                   bias=bt1[:, m:m + 1]).then_inc(s_relu, 1)
                    step += 1
            for n in range(2):
                for m in range(TOP2 // P):
                    act.wait_ge(s_top, step + 1)
                    act.activation(hidden2[:, TOP2 // P * n + m, :], banks[step % len(banks)][:, :], ACT.Relu,
                                   bias=bt2[:, m:m + 1]).then_inc(s_relu, 1)
                    step += 1
            for n in range(2):
                act.wait_ge(s_top, step + 1)
                act.copy(y_rows[n][0:1, :],
                         y2[n][0:1, :]).then_inc(s_row, 1)
                step += 1

        @block.vector
        def _(dve):
            wide = w0_wide.rearrange("p (f g) -> p f g", g=2 * FIELDS)
            raw = w0_raw.rearrange("p (f g) -> p f g", g=FIELDS)
            dve.wait_ge(s_w0, 16)
            for n in range(2):
                dve.tensor_tensor(wide[:, :, FIELDS * n:FIELDS * (n + 1)], raw, raw.rearrange("p f g -> p g f"),
                                  ALU.add).then_inc(s_sym, 1)
            dve.wait_ge(s_sym, 2)

            def diagonal(ap, width, start, count):
                return bass.AP(ap.tensor, ap.offset + start, [list(ap.ap[0]), [width + 1, count]])

            H = FIELDS // 2
            dve.tensor_copy(w0_dist[:, FIELDS:FIELDS * H].rearrange("p (d f) -> p d f", f=FIELDS),
                            bass.AP(w0_wide.tensor, w0_wide.offset + 1,
                                    [list(w0_wide.ap[0]), [1, H - 1], [2 * FIELDS + 1, FIELDS]])).then_inc(s_sym, 1)
            dve.tensor_copy(w0_dist[:, 0:FIELDS], diagonal(w0_raw, FIELDS, 0, FIELDS)).then_inc(s_sym, 1)
            dve.tensor_copy(w0_dist[:, FIELDS * H:FIELDS * H + H],
                            diagonal(w0_raw, FIELDS, H, H)).then_inc(s_sym, 1)
            dve.tensor_copy(w0_dist[:, FIELDS * H + H:FIELDS * (H + 1)],
                            diagonal(w0_raw, FIELDS, H * FIELDS, H)).then_inc(s_sym, 1)
            dve.wait_ge(s_sym, 6)
            once = w0_dist[:, FIELDS * H:FIELDS * (H + 1)]
            dve.tensor_copy(w0_dist[:, FIELDS * (H + 1):FIELDS * (H + GROUP)].rearrange("p (a f) -> p a f", f=FIELDS),
                            once.unsqueeze(1).to_broadcast([P, GROUP - 1, FIELDS])).then_inc(s_sym, 1)
            homes = [w0T_high[:, :, :], w0T_tail[:, :]]
            homes += [w1T[:, GROUP * g:GROUP * (g + 1), :] for g in range(GROUPS)]
            homes += [w2T_high[:, GROUP * g:GROUP * (g + 1), :] for g in range(GROUPS)]
            lows = {0: w0T_low[:, :, :]}
            lows.update({2 + GROUPS + g: w2T_low[:, GROUP * g:GROUP * (g + 1), :] for g in range(GROUPS)})
            for n, home in enumerate(homes):
                dve.wait_ge(s_turned, n + 1)
                source = prep[1][:, 0, :] if n == 1 else prep[n % 2]
                if n == 1:
                    dve.tensor_copy(home, source).then_inc(s_tail_w, 1)
                    dve.wait_ge(s_tail_w, 1)
                    for quarter in (1, 3):
                        lanes = slice(FIELDS * quarter, FIELDS * (quarter + 1))
                        last = dve.tensor_tensor(w0T_tail[lanes, :], source[lanes, :],
                                                 w0T_tail[lanes, :].bitcast(F32), ALU.subtract)
                    last.then_inc(s_stored, 1)
                elif n in lows:
                    dve.tensor_copy(home, source).then_inc(s_w_high, 1)
                    dve.wait_ge(s_w_high, sorted(lows).index(n) + 1)
                    dve.tensor_tensor(lows[n], source, home.bitcast(F32), ALU.subtract).then_inc(s_stored, 1)
                else:
                    dve.tensor_copy(home, source).then_inc(s_stored, 1)
            dve.wait_ge(s_biases, 5 * 16)
            dve.tensor_scalar(neg_last[:, :], bias_last[:, :], -1.0, None, ALU.mult).then_inc(s_neg, 1)
            dve.tensor_scalar(last_tiles[:, :], bias_last[:, :], float(TILES_PER_BLOCK), None, ALU.mult).then_inc(s_neg, 1)
            dve.wait_ge(s_neg, 2)
            dve.wait_ge(s_stored, PREP_GROUPS)
            dve.sem_inc(s_sum2, 1)
            dve.sem_inc(s_z, 1)

            def multiply(s, item):
                layer, n = item
                t = after(s, {0: 1, 1: 0, 2: -1}[layer])
                if item == (0, 0):
                    dve.wait_ge(s_shifted, 16 * GROUP * (number(t) + 1))
                    dve.wait_ge(s_xT, number(t) + 1)
                if item == TAIL:
                    dve.wait_ge(s_shifted_tail, 16 * GROUP * (number(t) + 1))
                    dve.wait_ge(s_tail_low, number(t))
                    dve.tensor_tensor(tail[:, :], shifted_tail[:, :], xT[:, :], ALU.mult).then_inc(s_tail, 1)
                    return
                x = shifted if layer == 0 else spread[t[1] % 2]
                b = (xT, h0[t[1] % 2], h1)[layer]
                if layer == 1:
                    if n == 0:
                        dve.wait_ge(s_h0, number(t) + 1)
                    if n % (GROUP // ITEM) == 0:
                        dve.wait_ge(s_spread[t[1] % 2][n // (GROUP // ITEM)], 32 * uses_of_parity(t))
                if item == (2, 0):
                    dve.wait_ge(s_h1, number(t) + 1)
                e, kind = plan.entry(s, item), kind_of(item)
                if not isinstance(e, int) or e >= RING[kind]:
                    dve.wait_ge(s_used[kind], e - RING[kind] + 1)
                r = plan.place(s, item, RING)
                z = prod[r][:, :, :] if kind == WHOLE else unsplit[kind][r][:, :, :]
                dve.tensor_tensor(z, x[:, ITEM * n:ITEM * (n + 1), :],
                                  b[:, :].unsqueeze(1).to_broadcast([P, ITEM, COLS]), ALU.mult).then_inc(s_made[kind], 1)

            def split_low(s, item):
                e, kind = plan.entry(s, item), BY_DVE
                dve.wait_ge(s_high[kind], e + 1)
                r = plan.place(s, item, RING)
                dve.tensor_tensor(low[kind][r][:, :, :], unsplit[kind][r][:, :, :],
                                  high[kind][r][:, :, :].bitcast(F32), ALU.subtract).then_inc(s_low[kind], 1)

            def first_of_block(t, col):
                if t[1] % TILES_PER_BLOCK:
                    return False
                b = t[0] + t[1] // TILES_PER_BLOCK
                if not isinstance(b, int) or b > 0:
                    dve.wait_ge(s_z, 2 * b + col)
                return True

            def add_kept(t):
                dve.wait_ge(s_kept0, number(t) + 1)
                dve.wait_ge(s_kept1, number(t) + 1)
                z = kept[t[1] % 2]
                if first_of_block(t, 0):
                    dve.tensor_copy(acc_kept[:, :], z[:, :]).then_inc(s_sum_kept, 1)
                else:
                    dve.wait_ge(s_sum_kept, number(t))
                    dve.tensor_tensor(acc_kept[:, :], acc_kept[:, :], z[:, :], ALU.add).then_inc(s_sum_kept, 1)

            def add_last(t):
                dve.wait_ge(s_used[kind_of(LAST2)], plan.entry(after(t, 1), LAST2) + 1)
                y = y2[t[1] % 2]
                if first_of_block(t, 1):
                    dve.tensor_scalar(acc_last[:, :], y[:, :], neg_last[:, :], last_tiles[:, :],
                                      ALU.max, ALU.add).then_inc(s_sum2, 1)
                else:
                    dve.wait_ge(s_sum2, number(t) + 1)
                    dve.scalar_tensor_tensor(out=acc_last[:, :], in0=y[:, :], scalar=neg_last[:, :],
                                             in1=acc_last[:, :], op0=ALU.max, op1=ALU.add).then_inc(s_sum2, 1)

            def fold(acc, z, t):
                b = t[0] + t[1] // TILES_PER_BLOCK
                dve.tensor_reduce(z[:, bass.ds(P * b, P)], acc[:, :].rearrange("p (e b) -> p b e", b=P),
                                  AXIS.X, ALU.add).then_inc(s_z, 1)

            def fold_kept(t):
                if t[1] % TILES_PER_BLOCK == TILES_PER_BLOCK - 1:
                    dve.wait_ge(s_sum_kept, number(t) + 1)
                    fold(acc_kept, z_kept, t)

            def fold_last(t):
                if t[1] % TILES_PER_BLOCK == TILES_PER_BLOCK - 1:
                    dve.wait_ge(s_sum2, number(t) + 1 + 1)
                    fold(acc_last, z_last, t)

            def slot(s):
                waiting = None
                items = plan.items(s)
                for item in items:
                    mine = item != TAIL and kind_of(item) == BY_DVE
                    multiply(s, item)
                    if waiting:
                        split_low(s, waiting)
                    waiting = item if mine else None
                    if (2, 0) in items and item == ADD_KEPT_AFTER:
                        add_kept(after(s, -1))
                    if (2, 0) in items and item == FOLD_KEPT_AFTER:
                        fold_kept(after(s, -1))
                    if item == (2, 3) and s[1] >= START:
                        add_last(after(s, -2))
                    if item == (2, 4) and s[1] >= START:
                        fold_last(after(s, -2))
                if waiting:
                    split_low(s, waiting)

            for k in range(-1, START):
                slot((0, k))
            with dve.Fori(0, BLOCKS - 1) as i:
                for k in range(START, START + TILES_PER_BLOCK):
                    slot((i, k))
            for k in range(START, TILES_PER_BLOCK + 1):
                slot((BLOCKS - 1, k))
            add_last((BLOCKS - 1, TILES_PER_BLOCK - 1))
            fold_last((BLOCKS - 1, TILES_PER_BLOCK - 1))


TABLES = FIELDS


def kernel(**inputs):
    import numpy as np
    import concourse.bacc as bacc
    from concourse.bass_utils import run_bass_kernel_spmd

    nc = bacc.Bacc("TRN2", target_bir_lowering=False, num_devices=1)
    arrays = {}

    def dram(name):
        a = np.ascontiguousarray(inputs[name])
        arrays["in_" + name] = a
        return nc.dram_tensor("in_" + name, a.shape, mybir.dt.from_np(a.dtype), kind="ExternalInput").ap()

    batch = inputs["ids"].shape[0]
    tiles = batch // P * TILES_PER_BLOCK
    tables = [dram(f"tbl_{f}") for f in range(TABLES)]
    xcols = nc.dram_tensor("xcols", (tiles, XROWS, COLS), F32, kind="Internal").ap()
    out = nc.dram_tensor("out", (batch, 1), F32, kind="ExternalOutput").ap()
    dlrm_tower(nc, dram("dense_ctx"), dram("ids"), tables, dram("W_top1"), dram("b_top1"),
               dram("W_top2"), dram("b_top2"), dram("W_top3"), dram("L0_rec_W0"), dram("L0_rec_b0"),
               dram("L0_rec_W1"), dram("L0_rec_b1"), dram("L0_rec_W2"), dram("L0_rec_b2"), xcols, out)
    result = run_bass_kernel_spmd(nc, [arrays], core_ids=[0])
    return result.results[0]["out"]
```
